# Optimizing a Trainium2 kernel written in Bass

```python
import numpy as np
import jax
import jax.numpy as jnp

def _softmax(x, axis=-1):
    return jax.nn.softmax(x, axis=axis)

def _gelu(x):
    return jax.nn.gelu(x, approximate=True)

def _silu(x):
    return jax.nn.silu(x)

def _sigmoid(x):
    return jax.nn.sigmoid(x)

def _layernorm(x, axis=-1, eps=1e-05):
    m = jnp.mean(x, axis=axis, keepdims=True)
    v = jnp.var(x, axis=axis, keepdims=True)
    return (x - m) / jnp.sqrt(v + eps)

def _scatter_add(tgt, idx, src, axis=0):
    return tgt.at[idx].add(src)

def _segment_sum(src, seg, n):
    return jax.ops.segment_sum(src, seg, n)
kernel_name = 'mk_adaln_ffn_d1_seqx_r4_fa0594'

def setup_inputs(seed: int=0):
    np.random.seed(seed)
    _w = jnp.asarray

    def _rec_inputs():
        import jax
        import jax.numpy as jnp
        _rk = jax.random.key(seed)
        x = -0.000125 + 0.9999 * jax.random.normal(jax.random.fold_in(_rk, 1), (32, 64, 1024), jnp.float32)
        _lenS = 64 - jax.random.randint(jax.random.fold_in(_rk, 7), (32,), 0, max(1, 64 // 4) + 1, jnp.int32)
        _lenS2 = 64 - jax.random.randint(jax.random.fold_in(_rk, 8), (32,), 0, max(1, 64 // 4) + 1, jnp.int32)
        cond_128 = 0.0061147 + 1.02565 * jax.random.normal(jax.random.fold_in(_rk, 11), (32, 128), jnp.float32)
        return (x, cond_128)
    x, cond_128 = _rec_inputs()

    def _L0_cond_setup():
        import jax, jax.numpy as jnp
        import numpy as np
        K = 8
        T = 1.0
        D_EMBD = 128
        IN_C = 64
        OUT_C = 64
        BS = 32
        H = 1024
        HID = 128
        key = jax.random.key(seed)
        ks = jax.random.split(key, 10)
        s = lambda fan_in: 1.0 / np.sqrt(fan_in)
        return {'x': jax.random.normal(ks[0], (BS, IN_C, H), dtype=jnp.float32), 'embedding': jax.random.normal(ks[1], (BS, D_EMBD), dtype=jnp.float32), 'W0': jax.random.normal(ks[2], (D_EMBD, HID), dtype=jnp.float32) * s(D_EMBD), 'b0': jnp.zeros((HID,), dtype=jnp.float32), 'W1': jax.random.normal(ks[3], (HID, HID), dtype=jnp.float32) * s(HID), 'b1': jnp.zeros((HID,), dtype=jnp.float32), 'W2': jax.random.normal(ks[4], (HID, K), dtype=jnp.float32) * s(HID), 'b2': jnp.zeros((K,), dtype=jnp.float32), 'weight': jax.random.normal(ks[5], (K, OUT_C, IN_C, 1), dtype=jnp.float32) * s(IN_C), 'bias_k': jax.random.normal(ks[6], (K, OUT_C), dtype=jnp.float32) * 0.1}
    _L0_cond_all = _L0_cond_setup()
    _L0_cond_in = {k: v for k, v in _L0_cond_all.items() if k in ('W0', 'b0', 'W1', 'b1', 'W2', 'b2', 'weight', 'bias_k')}
    del _L0_cond_all

    def _L0_ffn_setup():
        import jax, jax.numpy as jnp
        import numpy as np
        E = 8
        R = 8
        DIN = 1024
        DOUT = 1024
        TOP_K = 2
        SCALING = 2.0

        def _moe_lora(xf, gate_W, A, B):
            gate_probs = jax.nn.softmax(xf @ gate_W.T, axis=-1)
            weights, sel = jax.lax.top_k(gate_probs, TOP_K)
            weights = weights / jnp.sum(weights, axis=-1, keepdims=True)
            T = xf.shape[0]
            w_dense = jnp.zeros((T, E), xf.dtype).at[jnp.arange(T)[:, None], sel].add(weights)
            h = jnp.einsum('td,erd->ter', xf, A)
            h = h * (w_dense[:, :, None] * SCALING)
            return jnp.einsum('ter,eor->to', h, B)
        key = jax.random.key(seed)
        k0, k1, k2, k3, k4 = jax.random.split(key, 5)
        x = jax.random.normal(k0, (4, 512, DIN), jnp.float32)
        W_base = jax.random.normal(k1, (DOUT, DIN), jnp.float32) * 0.02
        gate_W = jax.random.normal(k2, (E, DIN), jnp.float32) * 0.02
        A = jax.random.normal(k3, (E, R, DIN), jnp.float32) * 0.02
        B = jax.random.normal(k4, (E, DOUT, R), jnp.float32) * 0.02
        return {'x': x, 'W_base': W_base, 'gate_W': gate_W, 'A': A, 'B': B}
    _L0_ffn_all = _L0_ffn_setup()
    _L0_ffn_in = {k: v for k, v in _L0_ffn_all.items() if k in ('W_base', 'gate_W', 'A', 'B')}
    del _L0_ffn_all
    return {'x': x, 'cond_128': cond_128, 'L0_cond_W0': _L0_cond_in['W0'], 'L0_cond_b0': _L0_cond_in['b0'], 'L0_cond_W1': _L0_cond_in['W1'], 'L0_cond_b1': _L0_cond_in['b1'], 'L0_cond_W2': _L0_cond_in['W2'], 'L0_cond_b2': _L0_cond_in['b2'], 'L0_cond_weight': _L0_cond_in['weight'], 'L0_cond_bias_k': _L0_cond_in['bias_k'], 'L0_ffn_W_base': _L0_ffn_in['W_base'], 'L0_ffn_gate_W': _L0_ffn_in['gate_W'], 'L0_ffn_A': _L0_ffn_in['A'], 'L0_ffn_B': _L0_ffn_in['B']}

def reference(x, cond_128, L0_cond_W0, L0_cond_b0, L0_cond_W1, L0_cond_b1, L0_cond_W2, L0_cond_b2, L0_cond_weight, L0_cond_bias_k, L0_ffn_W_base, L0_ffn_gate_W, L0_ffn_A, L0_ffn_B):
    import jax
    import jax.numpy as jnp

    def _L0_cond_ref(x, embedding, W0, b0, W1, b1, W2, b2, weight, bias_k):
        import jax, jax.numpy as jnp
        import numpy as np
        K = 8
        T = 1.0
        D_EMBD = 128
        IN_C = 64
        OUT_C = 64
        BS = 32
        H = 1024
        HID = 128
        h = jax.nn.gelu(embedding @ W0 + b0, approximate=False)
        h = jax.nn.gelu(h @ W1 + b1, approximate=False)
        att = jax.nn.softmax((h @ W2 + b2) / T, axis=-1)
        agg_w = jnp.einsum('bk,koi->boi', att, weight[..., 0])
        agg_b = att @ bias_k
        out = jnp.einsum('boi,bih->boh', agg_w, x) + agg_b[:, :, None]
        return out

    def _L0_ffn_ref(x, W_base, gate_W, A, B):
        import jax, jax.numpy as jnp
        import numpy as np
        E = 8
        R = 8
        DIN = 1024
        DOUT = 1024
        TOP_K = 2
        SCALING = 2.0

        def _moe_lora(xf, gate_W, A, B):
            gate_probs = jax.nn.softmax(xf @ gate_W.T, axis=-1)
            weights, sel = jax.lax.top_k(gate_probs, TOP_K)
            weights = weights / jnp.sum(weights, axis=-1, keepdims=True)
            T = xf.shape[0]
            w_dense = jnp.zeros((T, E), xf.dtype).at[jnp.arange(T)[:, None], sel].add(weights)
            h = jnp.einsum('td,erd->ter', xf, A)
            h = h * (w_dense[:, :, None] * SCALING)
            return jnp.einsum('ter,eor->to', h, B)
        xf = x.reshape(-1, x.shape[-1])
        out = xf @ W_base.T + _moe_lora(xf, gate_W, A, B)
        return out.reshape(*x.shape[:-1], DOUT)
    x = x + _L0_ffn_ref(_L0_cond_ref(x, cond_128, L0_cond_W0, L0_cond_b0, L0_cond_W1, L0_cond_b1, L0_cond_W2, L0_cond_b2, L0_cond_weight, L0_cond_bias_k), L0_ffn_W_base, L0_ffn_gate_W, L0_ffn_A, L0_ffn_B)
    return x

_drawn_inputs = setup_inputs


def setup_inputs(seed=0):
    import zlib

    import numpy as np

    out = dict(_drawn_inputs(seed))
    spreads = {'L0_cond_b0': (0.0, 0.722), 'L0_cond_b1': (0.0, 0.458), 'L0_cond_b2': (0.0, 0.415)}
    factors = {'L0_ffn_gate_W': 3.503, 'L0_ffn_A': 3.034, 'L0_ffn_B': 3.038}
    for name, (base, spread) in spreads.items():
        noise = np.random.default_rng([zlib.crc32(name.encode()), seed]).standard_normal(out[name].shape)
        drawn = base * np.exp(spread * noise) if base else spread * noise
        out[name] = jnp.asarray(drawn.astype(out[name].dtype))
    for name, factor in factors.items():
        out[name] = (out[name] * factor).astype(out[name].dtype)
    return out
```

```python
import concourse.bass as bass
from concourse import mybir
from contextlib import ExitStack

F32 = mybir.dt.float32
F32R = mybir.dt.float32r
U32 = mybir.dt.uint32
I32 = mybir.dt.int32
ACT = mybir.ActivationFunctionType
ALU = mybir.AluOpType
AX = mybir.AxisListType

P = 128
BATCH, CH, D = 32, 64, 1024
TOK = BATCH * CH
TILES = TOK // P
PAIRS = TILES // 2
KC = D // P
HC = KC // 2
K = 8
E, R = 8, 8
ER = E * R
SCALING = 2.0
HID = 128
GZ = E + ER
OG = P // K
NG = CH // OG

WIDTH = [364, 366, 366]
FIRST = [0, 364, 730]
NCOL = GZ + D
assert sum(WIDTH) == NCOL
SKIP = [GZ, 0, 0]
OUT0 = [0, WIDTH[0] - GZ, WIDTH[0] - GZ + WIDTH[1]]
OUTN = [WIDTH[0] - GZ, WIDTH[1], WIDTH[2]]
HT0 = 384

C_EMB, C_W0, C_W1, C_W2 = 0, 32, 160, 288
C_B0, C_B1, C_B2 = 296, 297, 298
C_MLP = 306
C_BK = 306
C_WL = 370
C_ALL = C_WL + NG * P

X_SLOTS = 4
W_PIECES = 6
W_SLOTS = 3
W_STAGE = HC * max(WIDTH)


def build(nc, x, wext, bt, small, scratch, out):
    x_t = x.rearrange("b c h -> (b c) h").rearrange("(t p) h -> t p h", p=P)
    out_t = out.rearrange("b c h -> (b c) h").rearrange("(t p) h -> t p h", p=P)

    with ExitStack() as ctx:
        def sb(name, shape, dt=F32):
            return ctx.enter_context(nc.sbuf_tensor(name, shape, dt))

        def sem(name):
            return ctx.enter_context(nc.semaphore(name))

        w_hi = sb("w_hi", [P, KC * NCOL], F32R)
        w_lo = sb("w_lo", [P, KC * NCOL], F32R)
        w_stage = sb("w_stage", [P, W_SLOTS, W_STAGE])
        b_hi = sb("b_hi", [P, D], F32R)
        b_lo = sb("b_lo", [P, D], F32R)
        x_raw = sb("x_raw", [P, X_SLOTS * D])
        x_hi = sb("x_hi", [P, 2, D], F32R)
        x_lo = sb("x_lo", [P, 2, D], F32R)
        y_full = sb("y_full", [P, 2, HC * P])
        y_hi = sb("y_hi", [P, 2, D], F32R)
        y_lo = sb("y_lo", [P, 2, D], F32R)
        out_sb = sb("out_sb", [P, 2, D])
        agg_hi = sb("agg_hi", [P, TILES * P], F32R)
        agg_lo = sb("agg_lo", [P, TILES * P], F32R)
        bias_all = sb("bias_all", [P, TOK])
        par = sb("par", [P, C_ALL])
        act_g = sb("act_g", [P, 2, BATCH])
        ones_row = sb("ones_row", [1, BATCH])
        att_max = sb("att_max", [BATCH, 1])
        att_exp = sb("att_exp", [BATCH, K])
        att_sum = sb("att_sum", [BATCH, 1])
        att_inv = sb("att_inv", [BATCH, 1])
        att_rep = sb("att_rep", [BATCH, OG, K])
        att_t = sb("att_t", [P, BATCH])
        att_diag = sb("att_diag", [P, OG, BATCH])
        aggb = sb("aggb", [BATCH, CH])
        ident32 = sb("ident32", [BATCH, BATCH])
        group_mask = sb("group_mask", [P, OG])
        ident = sb("ident", [P, P])
        ident_r = sb("ident_r", [P, P], F32R)
        expert_i = sb("expert_i", [P, E], I32)
        expert_no = sb("expert_no", [P, E])
        z_a = sb("z_a", [P, ER])
        top = sb("top", [P, 8])
        top_at = sb("top_at", [P, 8], U32)
        onehot = sb("onehot", [P, 2, E])
        ratio = sb("ratio", [P, 1])
        denom = sb("denom", [P, 1])
        weight = sb("weight", [P, 2])
        gate_a = sb("gate_a", [P, E])
        gate = sb("gate", [P, E])
        lora = sb("lora", [P, ER])
        lora_split = sb("lora_split", [P, 2, ER], F32R)
        lora_t = sb("lora_t", [P, P], F32R)

        main = [[ctx.enter_context(nc.psum_tensor(f"main{s}_{g}", [P, 512], F32)) for g in range(3)]
                for s in range(2)]
        yt = [ctx.enter_context(nc.psum_tensor(f"yt{h}", [P, 512], F32)) for h in range(2)]

        mlp_loaded = sem("mlp_loaded")
        par_loaded = sem("par_loaded")
        bt_loaded = sem("bt_loaded")
        x_loaded = [sem("x_loaded_even"), sem("x_loaded_odd")]
        w_loaded = [sem(f"w_loaded{s}") for s in range(W_SLOTS)]
        bias_stored = sem("bias_stored")
        bias_loaded = sem("bias_loaded")
        out_stored = [sem("out_stored_even"), sem("out_stored_odd")]
        consts = sem("consts")
        zeros_ready = sem("zeros_ready")
        expert_ready = sem("expert_ready")
        ident_ready = sem("ident_ready")
        mlp_mm = sem("mlp_mm")
        mlp_g = sem("mlp_g")
        att_step = sem("att_step")
        att_exped = sem("att_exped")
        att_mm = sem("att_mm")
        diag_ready = sem("diag_ready")
        aggb_mm = sem("aggb_mm")
        aggb_ready = sem("aggb_ready")
        agg_mm = sem("agg_mm")
        agg_hi_ready = sem("agg_hi_ready")
        agg_lo_ready = sem("agg_lo_ready")
        w_hi_ready = sem("w_hi_ready")
        w_lo_ready = sem("w_lo_ready")
        b_hi_ready = sem("b_hi_ready")
        b_lo_ready = sem("b_lo_ready")
        x_hi_ready = sem("x_hi_ready")
        x_lo_ready = sem("x_lo_ready")
        yt_done = sem("yt_done")
        y_added = sem("y_added")
        y_hi_ready = sem("y_hi_ready")
        y_lo_ready = sem("y_lo_ready")
        z_done = sem("z_done")
        gate_step = sem("gate_step")
        ratio_ready = sem("ratio_ready")
        lora_t_mm = sem("lora_t_mm")
        lora_t_ready = sem("lora_t_ready")
        main_done = sem("main_done")
        evacuated = sem("evacuated")

        GATE_STEPS = 12

        def w_cols(w, g, k):
            at = KC * FIRST[g] + k * WIDTH[g]
            return w[:, at:at + WIDTH[g]]

        def piece(w, n):
            g, half = n // 2, n % 2
            at = KC * FIRST[g] + half * HC * WIDTH[g]
            return w[:, at:at + HC * WIDTH[g]]

        def stage(n):
            return w_stage[:, n % W_SLOTS, 0:HC * WIDTH[n // 2]]

        def x_slot(t):
            return x_raw[:, bass.ds((t % X_SLOTS) * D, D)]

        block = ctx.enter_context(nc.Block())

        @block.sync
        def _(sp):
            sp.dma_start(par[:, 0:C_MLP], small[:, 0:C_MLP]).then_inc(mlp_loaded, 16)
            sp.dma_start(par[:, C_MLP:C_ALL], small[:, C_MLP:C_ALL]).then_inc(par_loaded, 16)

            def load_x(t, parity):
                sp.dma_start(x_slot(t), x_t[t]).then_inc(x_loaded[parity], 16)

            load_x(0, 0)
            for n in range(W_SLOTS):
                sp.dma_start(stage(n), piece(wext, n)).then_inc(w_loaded[n % W_SLOTS], 16)
            load_x(1, 1)
            for n in range(W_SLOTS, W_PIECES):
                sp.wait_ge(w_hi_ready, n - W_SLOTS + 1)
                sp.wait_ge(w_lo_ready, n - W_SLOTS + 1)
                sp.dma_start(stage(n), piece(wext, n)).then_inc(w_loaded[n % W_SLOTS], 16)
            for half in range(2):
                sp.dma_start(out_sb[half * ER:(half + 1) * ER, 0, :], bt).then_inc(bt_loaded, 16)
            sp.wait_ge(x_loaded[0], 16)
            load_x(2, 0)

            def step(j, parity, load=True):
                t = 2 * j + parity
                sp.wait_ge(evacuated, 3 * t)
                sp.dma_start(out_t[t - 1], out_sb[:, 1 - parity, :]).then_inc(out_stored[1 - parity], 16)
                if load:
                    sp.wait_ge(x_loaded[1 - parity], (j + parity + 1) * 16)
                    load_x(t + 3, 1 - parity)

            sp.wait_ge(x_loaded[1], 16)
            load_x(3, 1)
            step(0, 1)
            with sp.Fori(1, PAIRS - 2) as j:
                step(j, 0)
                step(j, 1)
            step(PAIRS - 2, 0)
            for t in range(TILES - 3, TILES + 1):
                step(t // 2, t % 2, load=False)
            sp.wait_ge(out_stored[0], TILES // 2 * 16)
            sp.wait_ge(out_stored[1], TILES // 2 * 16)

        @block.gpsimd
        def _(pool):
            nc.gpsimd.memset(ones_row[:, :], 1.0).then_inc(consts, 1)
            nc.gpsimd.memset(ident32[:, :], 0.0).then_inc(consts, 1)
            nc.gpsimd.memset(group_mask[:, :], 1.0).then_inc(consts, 1)
            nc.gpsimd.memset(ident[:, :], 0.0).then_inc(consts, 1)
            pool.wait_ge(consts, 4)
            nc.gpsimd.affine_select(out=ident32[:, :], in_=ident32[:, :], compare_op=ALU.not_equal, fill=1.0,
                                    base=0, pattern=[[-1, BATCH]], channel_multiplier=1).then_inc(consts, 1)
            nc.gpsimd.affine_select(out=group_mask[:, :], in_=group_mask[:, :], compare_op=ALU.is_ge, fill=0.0,
                                    base=0, pattern=[[-K, OG]], channel_multiplier=1).then_inc(consts, 1)
            pool.wait_ge(consts, 6)
            nc.gpsimd.affine_select(out=group_mask[:, :], in_=group_mask[:, :], compare_op=ALU.is_ge, fill=0.0,
                                    base=K - 1, pattern=[[K, OG]], channel_multiplier=-1).then_inc(consts, 1)
            nc.gpsimd.memset(agg_hi[:, :].bitcast(U32), 0).then_inc(zeros_ready, 1)
            nc.gpsimd.memset(agg_lo[:, :].bitcast(U32), 0).then_inc(zeros_ready, 1)
            nc.gpsimd.affine_select(out=ident[:, :], in_=ident[:, :], compare_op=ALU.not_equal, fill=1.0,
                                    base=0, pattern=[[-1, P]], channel_multiplier=1).then_inc(consts, 1)
            nc.gpsimd.iota(expert_i[:, :], pattern=[[1, E]], base=0, channel_multiplier=0).then_inc(consts, 1)
            pool.wait_ge(consts, 9)
            nc.gpsimd.tensor_copy(expert_no[:, :], expert_i[:, :]).then_inc(expert_ready, 1)

            def x_low(t, parity):
                pool.wait_ge(x_hi_ready, t + 1)
                nc.gpsimd.tensor_tensor(x_lo[:, parity, :], x_slot(t), x_hi[:, parity, :].bitcast(F32),
                                        ALU.subtract).then_inc(x_lo_ready, 1)

            def y_low(t, parity):
                for h in range(2):
                    pool.wait_ge(y_hi_ready, 2 * t + h + 1)
                    cols = slice(h * HC * P, (h + 1) * HC * P)
                    nc.gpsimd.tensor_tensor(y_lo[:, parity, cols], y_full[:, h, :],
                                            y_hi[:, parity, cols].bitcast(F32),
                                            ALU.subtract).then_inc(y_lo_ready, 1)

            def step(j, parity):
                t = 2 * j + parity
                x_low(t + 1, 1 - parity)
                y_low(t + 1, 1 - parity)

            x_low(0, 0)
            y_low(0, 0)
            step(0, 0)
            step(0, 1)
            with pool.Fori(1, PAIRS - 1) as j:
                step(j, 0)
                step(j, 1)
            step(PAIRS - 1, 0)

        @block.scalar
        def _(act):
            nc.scalar.preload_act_table(ACT.Gelu)
            act.wait_ge(mlp_loaded, 16)
            for layer, bias in ((0, C_B0), (1, C_B1)):
                act.wait_ge(mlp_mm, layer + 1)
                nc.scalar.activation(act_g[:, layer, :], yt[0][:, BATCH * layer:BATCH * (layer + 1)], ACT.Gelu,
                                     bias=par[:, bias:bias + 1]).then_inc(mlp_g, 1)
            nc.scalar.preload_act_table(ACT.Exp)
            act.wait_ge(att_step, 1)
            nc.scalar.activation(att_exp[:, :], yt[0][0:BATCH, 64:64 + K], ACT.Exp, bias=att_max[:, 0:1],
                                 accum_out=att_sum[:, 0:1]).then_inc(att_exped, 1)

            def x_high(j, parity, first=False):
                t = 2 * j + parity
                act.wait_ge(x_loaded[parity], (j + 1) * 16)
                if not first:
                    act.wait_ge(yt_done, 2 * (t - 1))
                nc.scalar.activation(x_hi[:, parity, :], x_slot(t), ACT.Copy).then_inc(x_hi_ready, 1)

            def y_high(t, parity, first=False):
                for h in range(2):
                    act.wait_ge(y_added, 2 * t + h + 1)
                    if h == 0 and not first:
                        act.wait_ge(main_done, t - 1)
                    nc.scalar.activation(y_hi[:, parity, h * HC * P:(h + 1) * HC * P], y_full[:, h, :],
                                         ACT.Copy).then_inc(y_hi_ready, 1)

            act.wait_ge(aggb_ready, 1)
            act.dma_start(scratch, aggb[:, :]).then_inc(bias_stored, 16)
            x_high(0, 0, first=True)
            act.wait_ge(zeros_ready, 2)
            for g in range(NG):
                act.wait_ge(agg_mm, g + 1)
                for s in range(2):
                    rows = slice(CH * s, CH * (s + 1))
                    dst = agg_hi[rows, :].rearrange("p (t c) -> p t c", c=P)
                    src = main[0][g][rows, :] if g < 3 else main[1][0][rows, :]
                    src = src.rearrange("p (o t s) -> p t o s", o=OG, s=2)[:, :, :, s]
                    nc.scalar.activation(dst[:, :, CH * s + OG * g:CH * s + OG * (g + 1)], src,
                                         ACT.Copy).then_inc(agg_hi_ready, 1)
            act.wait_ge(bias_stored, 16)
            act.dma_start(bias_all[:, :], scratch.rearrange("b c -> (b c)").partition_broadcast(P))\
               .then_inc(bias_loaded, 16)
            act.wait_ge(consts, 8)
            nc.scalar.activation(ident_r[:, :], ident[:, :], ACT.Copy).then_inc(ident_ready, 1)
            for n in range(W_PIECES):
                if n == 2:
                    y_high(0, 0, first=True)
                act.wait_ge(w_loaded[n % W_SLOTS], (n // W_SLOTS + 1) * 16)
                nc.scalar.activation(piece(w_hi, n), stage(n), ACT.Copy).then_inc(w_hi_ready, 1)
            act.wait_ge(bt_loaded, 32)
            nc.scalar.activation(b_hi[:, :], out_sb[:, 0, :], ACT.Copy).then_inc(b_hi_ready, 1)

            def step(j, parity, first=False, last=False):
                t = 2 * j + parity
                if not last:
                    x_high(j + parity, 1 - parity, first=first)
                act.wait_ge(gate_step, GATE_STEPS * t + 2)
                nc.scalar.activation(ratio[:, 0:1], top[:, 0:1], ACT.Exp, bias=top[:, 1:2],
                                     scale=-1.0).then_inc(ratio_ready, 1)
                act.wait_ge(lora_t_mm, t + 1)
                nc.scalar.activation(lora_t[:, :], main[parity][0][:, HT0:HT0 + P],
                                     ACT.Copy).then_inc(lora_t_ready, 1)
                if not last:
                    y_high(t + 1, 1 - parity, first=first)

            step(0, 0, first=True)
            step(0, 1)
            with act.Fori(1, PAIRS - 1) as j:
                step(j, 0)
                step(j, 1)
            step(PAIRS - 1, 0)
            step(PAIRS - 1, 1, last=True)

        @block.vector
        def _(dve):
            dve.wait_ge(mlp_mm, 3)
            nc.vector.tensor_reduce(att_max[:, 0:1], yt[0][0:BATCH, 64:64 + K], AX.X, ALU.max,
                                    negate=True).then_inc(att_step, 1)
            dve.wait_ge(att_exped, 1)
            nc.vector.reciprocal(att_inv[:, :], att_sum[:, :]).then_inc(att_step, 1)
            dve.wait_ge(att_step, 2)
            nc.vector.tensor_scalar(att_rep[:, :, :], att_exp[:, None, :].to_broadcast([BATCH, OG, K]),
                                    att_inv[:, 0:1], None, ALU.mult).then_inc(att_step, 1)
            dve.wait_ge(att_mm, 1)
            nc.vector.tensor_copy(att_t[:, :], yt[1][:, 0:BATCH]).then_inc(att_step, 1)
            dve.wait_ge(att_step, 4)
            dve.wait_ge(consts, 7)
            nc.vector.tensor_tensor(att_diag[:, :, :], group_mask[:, :, None].to_broadcast([P, OG, BATCH]),
                                    att_t[:, None, :].to_broadcast([P, OG, BATCH]),
                                    ALU.mult).then_inc(diag_ready, 1)
            dve.wait_ge(aggb_mm, 1)
            nc.vector.tensor_copy(aggb[:, :], yt[1][0:BATCH, 64:64 + CH]).then_inc(aggb_ready, 1)
            for g in range(NG):
                for s in range(2):
                    dve.wait_ge(agg_hi_ready, 2 * g + s + 1)
                    rows = slice(CH * s, CH * (s + 1))
                    cols = slice(CH * s + OG * g, CH * s + OG * (g + 1))
                    hi = agg_hi[rows, :].rearrange("p (t c) -> p t c", c=P)[:, :, cols].bitcast(F32)
                    lo = agg_lo[rows, :].rearrange("p (t c) -> p t c", c=P)[:, :, cols]
                    src = main[0][g][rows, :] if g < 3 else main[1][0][rows, :]
                    src = src.rearrange("p (o t s) -> p t o s", o=OG, s=2)[:, :, :, s]
                    nc.vector.tensor_tensor(lo, src, hi, ALU.subtract).then_inc(agg_lo_ready, 1)

            def y_add(t, parity, first=False):
                for h in range(2):
                    dve.wait_ge(yt_done, 2 * t + h + 1)
                    if not first:
                        dve.wait_ge(y_lo_ready, 2 * t + h - 1)
                    bias = bias_all[:, bass.ds(t * P, P)][:, None, :].to_broadcast([P, HC, P])
                    nc.vector.tensor_tensor(y_full[:, h, :].rearrange("p (k c) -> p k c", c=P),
                                            yt[h][:, :].rearrange("p (k c) -> p k c", c=P), bias,
                                            ALU.add).then_inc(y_added, 1)

            for n in range(W_PIECES):
                if n == 2:
                    dve.wait_ge(bias_loaded, 16)
                    y_add(0, 0, first=True)
                dve.wait_ge(w_hi_ready, n + 1)
                nc.vector.tensor_tensor(piece(w_lo, n), stage(n), piece(w_hi, n).bitcast(F32),
                                        ALU.subtract).then_inc(w_lo_ready, 1)
            dve.wait_ge(b_hi_ready, 1)
            nc.vector.tensor_tensor(b_lo[:, :], out_sb[:, 0, :], b_hi[:, :].bitcast(F32),
                                    ALU.subtract).then_inc(b_lo_ready, 1)
            dve.wait_ge(expert_ready, 1)

            def gating(t, parity):
                base = GATE_STEPS * t
                z = main[parity][0]
                dve.wait_ge(z_done, t + 1)
                nc.vector.tensor_copy(z_a[:, :], z[:, E:GZ]).then_inc(gate_step, 1)
                nc.vector.max(top[:, :], z[:, 0:E]).then_inc(gate_step, 1)
                dve.wait_ge(ratio_ready, t + 1)
                nc.vector.tensor_scalar(denom[:, :], ratio[:, :], 1.0, 1.0 / SCALING,
                                        ALU.add, ALU.mult).then_inc(gate_step, 1)
                nc.vector.max_index(top_at[:, :], top[:, :], z[:, 0:E]).then_inc(gate_step, 1)
                dve.wait_ge(gate_step, base + 3)
                nc.vector.reciprocal(weight[:, 0:1], denom[:, :]).then_inc(gate_step, 1)
                dve.wait_ge(gate_step, base + 4)
                nc.vector.tensor_tensor(onehot[:, :, :], expert_no[:, None, :].to_broadcast([P, 2, E]),
                                        top_at[:, 0:2, None].to_broadcast([P, 2, E]),
                                        ALU.is_equal).then_inc(gate_step, 1)
                dve.wait_ge(gate_step, base + 5)
                nc.vector.tensor_tensor(weight[:, 1:2], weight[:, 0:1], ratio[:, :],
                                        ALU.mult).then_inc(gate_step, 1)
                dve.wait_ge(gate_step, base + 6)
                nc.vector.tensor_scalar(gate_a[:, :], onehot[:, 0, :], weight[:, 0:1], None,
                                        ALU.mult).then_inc(gate_step, 1)
                dve.wait_ge(gate_step, base + 8)
                nc.vector.scalar_tensor_tensor(gate[:, :], onehot[:, 1, :], weight[:, 1:2], gate_a[:, :],
                                               ALU.mult, ALU.add).then_inc(gate_step, 1)
                dve.wait_ge(gate_step, base + 9)
                nc.vector.tensor_tensor(lora[:, :].rearrange("p (e r) -> p e r", r=R),
                                        z_a[:, :].rearrange("p (e r) -> p e r", r=R),
                                        gate[:, :, None].to_broadcast([P, E, R]),
                                        ALU.mult).then_inc(gate_step, 1)
                dve.wait_ge(gate_step, base + 10)
                nc.vector.tensor_copy(lora_split[:, 0, :], lora[:, :]).then_inc(gate_step, 1)
                dve.wait_ge(gate_step, base + 11)
                nc.vector.tensor_tensor(lora_split[:, 1, :], lora[:, :], lora_split[:, 0, :].bitcast(F32),
                                        ALU.subtract).then_inc(gate_step, 1)

            def add_out(j, parity, first=False):
                t = 2 * j + parity
                dve.wait_ge(main_done, t + 1)
                if not first:
                    dve.wait_ge(out_stored[parity], j * 16)
                for g in range(3):
                    cols = slice(OUT0[g], OUT0[g] + OUTN[g])
                    nc.vector.tensor_tensor(out_sb[:, parity, cols],
                                            main[parity][g][:, SKIP[g]:SKIP[g] + OUTN[g]],
                                            x_raw[:, bass.ds((t % X_SLOTS) * D + OUT0[g], OUTN[g])],
                                            ALU.add).then_inc(evacuated, 1)

            def step(j, parity, early=False, first=False, last=False):
                t = 2 * j + parity
                if not first:
                    add_out(j - 1 + parity, 1 - parity, first=early)
                gating(t, parity)
                if not last:
                    y_add(t + 1, 1 - parity)

            step(0, 0, first=True)
            step(0, 1, early=True)
            step(1, 0, early=True)
            step(1, 1)
            with dve.Fori(2, PAIRS - 1) as j:
                step(j, 0)
                step(j, 1)
            step(PAIRS - 1, 0)
            step(PAIRS - 1, 1, last=True)
            add_out(PAIRS - 1, 1)

        @block.tensor
        def _(pe):
            pe.wait_ge(mlp_loaded, 16)
            nc.tensor.matmul(yt[0][:, 0:BATCH], par[:, C_W0:C_W0 + HID], par[:, C_EMB:C_EMB + BATCH],
                             start=True, stop=True).then_inc(mlp_mm, 1)
            pe.wait_ge(mlp_g, 1)
            nc.tensor.matmul(yt[0][:, BATCH:2 * BATCH], par[:, C_W1:C_W1 + HID], act_g[:, 0, :],
                             start=True, stop=True).then_inc(mlp_mm, 1)
            pe.wait_ge(mlp_g, 2)
            pe.wait_ge(consts, 1)
            nc.tensor.matmul(yt[0][0:BATCH, 64:64 + K], act_g[:, 1, :], par[:, C_W2:C_W2 + K],
                             start=True, stop=False)
            nc.tensor.matmul(yt[0][0:BATCH, 64:64 + K], ones_row[:, :], par[0:1, C_B2:C_B2 + K],
                             start=False, stop=True).then_inc(mlp_mm, 1)
            pe.wait_ge(att_step, 3)
            pe.wait_ge(consts, 5)
            nc.tensor.matmul(yt[1][:, 0:BATCH], att_rep[:, :, :].rearrange("b o k -> b (o k)"), ident32[:, :],
                             start=True, stop=True).then_inc(att_mm, 1)
            pe.wait_ge(att_step, 4)
            pe.wait_ge(par_loaded, 16)
            nc.tensor.matmul(yt[1][0:BATCH, 64:64 + CH], att_t[0:K, :], par[0:K, C_BK:C_BK + CH],
                             start=True, stop=True).then_inc(aggb_mm, 1)
            pe.wait_ge(diag_ready, 1)
            for g in range(NG):
                dst = main[0][g] if g < 3 else main[1][0]
                wl = par[:, C_WL + P * g:C_WL + P * (g + 1)]
                nc.tensor.matmul(dst[:, :], wl,
                                 att_diag[:, :, :].rearrange("p o b -> p (o b)"),
                                 start=True, stop=True).then_inc(agg_mm, 1)

            def make_yt(t, parity, first=False):
                pe.wait_ge(x_hi_ready, t + 1)
                pe.wait_ge(x_lo_ready, t + 1)
                a_hi = agg_hi[:, bass.ds(t * P, P)]
                a_lo = agg_lo[:, bass.ds(t * P, P)]
                for h in range(2):
                    if not first:
                        pe.wait_ge(y_added, 2 * t + h - 1)
                    for c in range(HC):
                        k = HC * h + c
                        hi = x_hi[:, parity, k * P:(k + 1) * P]
                        lo = x_lo[:, parity, k * P:(k + 1) * P]
                        dst = yt[h][:, c * P:(c + 1) * P]
                        nc.tensor.matmul(dst, hi, a_hi, start=True, stop=False)
                        nc.tensor.matmul(dst, hi, a_lo, start=False, stop=False)
                        last = nc.tensor.matmul(dst, lo, a_hi, start=False, stop=True)
                    last.then_inc(yt_done, 1)

            def group(t, parity, g, by_half, by_piece, chunks=range(KC)):
                for k in chunks:
                    if by_half and k % HC == 0:
                        pe.wait_ge(y_hi_ready, 2 * t + k // HC + 1)
                        pe.wait_ge(y_lo_ready, 2 * t + k // HC + 1)
                    if by_piece and k % HC == 0:
                        pe.wait_ge(w_hi_ready, 2 * g + k // HC + 1)
                        pe.wait_ge(w_lo_ready, 2 * g + k // HC + 1)
                    hi = y_hi[:, parity, k * P:(k + 1) * P]
                    lo = y_lo[:, parity, k * P:(k + 1) * P]
                    dst = main[parity][g][:, 0:WIDTH[g]]
                    nc.tensor.matmul(dst, hi, w_cols(w_hi, g, k), start=(k == 0), stop=False,
                                     skip_group_check=True)
                    nc.tensor.matmul(dst, hi, w_cols(w_lo, g, k), start=False, stop=False,
                                     skip_group_check=True)
                    last = nc.tensor.matmul(dst, lo, w_cols(w_hi, g, k), start=False, stop=(k == KC - 1),
                                            skip_group_check=True)
                return last

            def step(j, parity, early=False, first=False, last=False):
                t = 2 * j + parity
                if not (early or first):
                    pe.wait_ge(evacuated, 3 * (t - 1))
                group(t, parity, 0, by_half=True, by_piece=first).then_inc(z_done, 1)
                group(t, parity, 1, by_half=False, by_piece=first)
                if not last:
                    make_yt(t + 1, 1 - parity)
                group(t, parity, 2, by_half=False, by_piece=first, chunks=range(HC))
                if first:
                    pe.wait_ge(ident_ready, 1)
                pe.wait_ge(gate_step, GATE_STEPS * (t + 1))
                nc.tensor.matmul(main[parity][0][:, HT0:HT0 + P],
                                 lora_split[:, :, :].rearrange("p a c -> p (a c)"), ident_r[:, :],
                                 start=False, stop=False, skip_group_check=True).then_inc(lora_t_mm, 1)
                group(t, parity, 2, by_half=False, by_piece=first, chunks=range(HC, KC))
                if first:
                    pe.wait_ge(b_lo_ready, 1)
                pe.wait_ge(lora_t_ready, t + 1)
                for g in range(3):
                    for b in (b_hi, b_lo):
                        done = nc.tensor.matmul(main[parity][g][:, SKIP[g]:SKIP[g] + OUTN[g]], lora_t[:, :],
                                                b[:, OUT0[g]:OUT0[g] + OUTN[g]], start=False, stop=(b is b_lo),
                                                skip_group_check=True)
                done.then_inc(main_done, 1)

            pe.wait_ge(agg_hi_ready, 2 * NG)
            pe.wait_ge(agg_lo_ready, 2 * NG)
            make_yt(0, 0, first=True)
            step(0, 0, first=True)
            step(0, 1, early=True)
            with pe.Fori(1, PAIRS - 1) as j:
                step(j, 0)
                step(j, 1)
            step(PAIRS - 1, 0)
            step(PAIRS - 1, 1, last=True)


def kernel(**inputs):
    import numpy as np
    import concourse.bacc as bacc
    from concourse import mybir as mb
    from concourse.bass_utils import run_bass_kernel_spmd

    a = {k: np.asarray(v) for k, v in inputs.items()}
    wt = np.concatenate([a["L0_ffn_gate_W"], a["L0_ffn_A"].reshape(ER, D), a["L0_ffn_W_base"]], axis=0).T
    wt = wt.reshape(KC, P, NCOL).transpose(1, 0, 2)
    wext = np.concatenate([wt[:, :, f:f + n].reshape(P, KC * n) for f, n in zip(FIRST, WIDTH)], axis=1)
    bt = a["L0_ffn_B"].transpose(0, 2, 1).reshape(ER, D)
    small = np.zeros((P, C_ALL), np.float32)
    small[:, C_EMB:C_EMB + BATCH] = a["cond_128"].T
    small[:, C_W0:C_W0 + HID] = a["L0_cond_W0"]
    small[:, C_W1:C_W1 + HID] = a["L0_cond_W1"]
    small[:, C_W2:C_W2 + K] = a["L0_cond_W2"]
    small[:, C_B0] = a["L0_cond_b0"]
    small[:, C_B1] = a["L0_cond_b1"]
    small[0, C_B2:C_B2 + K] = a["L0_cond_b2"]
    small[0:K, C_BK:C_BK + CH] = a["L0_cond_bias_k"]
    wl = a["L0_cond_weight"].reshape(K, NG, OG, CH).transpose(2, 0, 1, 3)
    wl = wl.reshape(P, NG, 1, CH)
    small[:, C_WL:C_ALL] = np.concatenate([wl, wl], axis=2).reshape(P, NG * P)

    nc = bacc.Bacc("TRN2", target_bir_lowering=False, num_devices=1)
    arrays = {"x_in": a["x"], "wext_in": wext, "bt_in": bt, "small_in": small}
    arrays = {k: np.ascontiguousarray(v) for k, v in arrays.items()}
    aps = [nc.dram_tensor(k, v.shape, mb.dt.from_np(v.dtype), kind="ExternalInput").ap() for k, v in arrays.items()]
    scratch = nc.dram_tensor("bias_rows", (BATCH, CH), mb.dt.float32, kind="Internal").ap()
    out = nc.dram_tensor("out_0", (BATCH, CH, D), mb.dt.float32, kind="ExternalOutput").ap()
    build(nc, *aps, scratch, out)
    r = run_bass_kernel_spmd(nc, [arrays], core_ids=[0])
    return r.results[0]["out_0"]
```

```python
import concourse.bass as bass
from concourse import mybir
from contextlib import ExitStack

F32 = mybir.dt.float32
F32R = mybir.dt.float32r
U32 = mybir.dt.uint32
I32 = mybir.dt.int32
ACT = mybir.ActivationFunctionType
ALU = mybir.AluOpType
AX = mybir.AxisListType

P = 128
BATCH, CH, D = 32, 64, 1024
TOK = BATCH * CH
TILES = TOK // P
PAIRS = TILES // 2
KC = D // P
K = 8
E, R = 8, 8
ER = E * R
SCALING = 2.0
HID = 128
GZ = E + ER
OG = P // K
NG = CH // OG

G = 3
WIDTH = [364, 366, 366]
FIRST = [0, 364, 730]
NCOL = GZ + D
assert sum(WIDTH) == NCOL
SKIP = [GZ, 0, 0]
OUT0 = [0, WIDTH[0] - GZ, WIDTH[0] - GZ + WIDTH[1]]
OUTN = [WIDTH[0] - GZ, WIDTH[1], WIDTH[2]]

C_EMB, C_W0, C_W1, C_W2 = 0, 32, 160, 288
C_B0, C_B1, C_B2 = 296, 297, 298
C_MLP = 306
C_BK = 306
C_WL = C_BK + P
C_ALL = C_WL + NG * P

PC = 2
PIECES = G * KC // PC
PER_G = KC // PC


def build(nc, x, xt, wext, bt, small, out):
    x_t = x.rearrange("b c h -> (b c) h").rearrange("(t p) h -> t p h", p=P)
    out_t = out.rearrange("b c h -> (b c) h").rearrange("(t p) h -> t p h", p=P)

    with ExitStack() as ctx:
        def sb(name, shape, dt=F32):
            return ctx.enter_context(nc.sbuf_tensor(name, shape, dt))

        def ps(name):
            return ctx.enter_context(nc.psum_tensor(name, [P, 512], F32))

        def sem(name):
            return ctx.enter_context(nc.semaphore(name))

        w_raw = sb("w_raw", [P, KC * NCOL])
        w_hi = sb("w_hi", [P, KC * NCOL], F32R)
        w_lo = sb("w_lo", [P, KC * NCOL], F32R)
        fold = sb("fold", [P, PC * max(WIDTH)])
        w_part = sb("w_part", [P, NCOL])
        w_sum = sb("w_sum", [P, NCOL])
        b_hi = sb("b_hi", [P, D], F32R)
        b_lo = sb("b_lo", [P, D], F32R)
        xt_raw = sb("xt_raw", [P, 2, D])
        xt_hi = sb("xt_hi", [P, 2, D], F32R)
        xt_lo = sb("xt_lo", [P, 2, D], F32R)
        x_nat = sb("x_nat", [P, 2, D])
        z_hi = sb("z_hi", [P, NCOL], F32R)
        z_lo = sb("z_lo", [P, NCOL], F32R)
        out_sb = sb("out_sb", [P, 2, D])
        agg = sb("agg", [P, TILES, CH])
        blk_hi = sb("blk_hi", [P, 2, P], F32R)
        blk_lo = sb("blk_lo", [P, 2, P], F32R)
        bias = sb("bias", [P, TILES])
        par = sb("par", [P, C_ALL])
        act_g = sb("act_g", [P, 2, BATCH])
        ones = sb("ones", [P, P])
        att_max = sb("att_max", [BATCH, 1])
        att_exp = sb("att_exp", [BATCH, K])
        att_sum = sb("att_sum", [BATCH, 1])
        att_inv = sb("att_inv", [BATCH, 1])
        att_rep = sb("att_rep", [BATCH, OG, K])
        att_t = sb("att_t", [P, BATCH])
        att_diag = sb("att_diag", [P, OG, BATCH])
        ident32 = sb("ident32", [BATCH, BATCH])
        group_mask = sb("group_mask", [P, OG])
        ident = sb("ident", [P, P])
        ident_r = sb("ident_r", [P, P], F32R)
        expert_i = sb("expert_i", [P, E], I32)
        expert_no = sb("expert_no", [P, E])
        logits = sb("logits", [P, E])
        z_a = sb("z_a", [P, ER])
        top = sb("top", [P, 8])
        top_at = sb("top_at", [P, 8], U32)
        onehot = sb("onehot", [P, 2, E])
        ratio = sb("ratio", [P, 1])
        denom = sb("denom", [P, 1])
        weight = sb("weight", [P, 2])
        gate_a = sb("gate_a", [P, E])
        gate = sb("gate", [P, E])
        lora = sb("lora", [P, ER])
        lora_split = sb("lora_split", [P, 2, ER], F32R)
        lora_t = sb("lora_t", [P, P], F32R)

        z_ps = [ps(f"z_ps{g}") for g in range(G)]
        o_ps = [ps(f"o_ps{g}") for g in range(G)]
        t_ps = ps("t_ps")
        s_ps = ps("s_ps")

        mlp_loaded = sem("mlp_loaded")
        par_loaded = sem("par_loaded")
        bt_loaded = sem("bt_loaded")
        xt_loaded = [sem("xt_loaded_even"), sem("xt_loaded_odd")]
        xn_loaded = [sem("xn_loaded_even"), sem("xn_loaded_odd")]
        w_loaded = [sem(f"w_loaded{n}") for n in range(PIECES)]
        out_stored = [sem("out_stored_even"), sem("out_stored_odd")]
        consts = sem("consts")
        zeros_ready = sem("zeros_ready")
        expert_ready = sem("expert_ready")
        ident_ready = sem("ident_ready")
        mlp_mm = sem("mlp_mm")
        mlp_g = sem("mlp_g")
        att_step = sem("att_step")
        att_exped = sem("att_exped")
        att_mm = sem("att_mm")
        diag_ready = sem("diag_ready")
        bias_mm = sem("bias_mm")
        bias_ready = sem("bias_ready")
        agg_mm = sem("agg_mm")
        agg_ready = sem("agg_ready")
        w_hi_ready = sem("w_hi_ready")
        w_lo_ready = sem("w_lo_ready")
        fold_step = sem("fold_step")
        fold_g2 = sem("fold_g2")
        sum_mm = sem("sum_mm")
        sum_ready = sem("sum_ready")
        b_hi_ready = sem("b_hi_ready")
        b_lo_ready = sem("b_lo_ready")
        x_hi_ready = sem("x_hi_ready")
        x_lo_ready = sem("x_lo_ready")
        x_biased = sem("x_biased")
        z_done = sem("z_done")
        z_hi_ready = sem("z_hi_ready")
        z_lo_ready = sem("z_lo_ready")
        blk_hi_ready = sem("blk_hi_ready")
        blk_lo_ready = sem("blk_lo_ready")
        o_done = sem("o_done")
        gate_step = sem("gate_step")
        ratio_ready = sem("ratio_ready")
        lora_t_mm = sem("lora_t_mm")
        lora_t_ready = sem("lora_t_ready")
        main_done = sem("main_done")
        evacuated = sem("evacuated")

        GATE_STEPS = 13

        def w_cols(w, g, k):
            at = KC * FIRST[g] + k * WIDTH[g]
            return w[:, at:at + WIDTH[g]]

        def piece(w, n):
            g, q = n // PER_G, n % PER_G
            at = KC * FIRST[g] + q * PC * WIDTH[g]
            return w[:, at:at + PC * WIDTH[g]]

        def z_cols(z, g):
            return z[:, FIRST[g]:FIRST[g] + WIDTH[g]]

        block = ctx.enter_context(nc.Block())

        @block.sync
        def _(sp):
            def load_xt(t, parity):
                sp.dma_start(xt_raw[:, parity, :], xt[t]).then_inc(xt_loaded[parity], 16)

            def load_xn(t, parity):
                sp.dma_start(x_nat[:, parity, :], x_t[t]).then_inc(xn_loaded[parity], 16)

            sp.dma_start(par[:, 0:C_MLP], small[:, 0:C_MLP]).then_inc(mlp_loaded, 16)
            load_xt(0, 0)
            for n in range(PIECES):
                sp.dma_start(piece(w_raw, n), piece(wext, n)).then_inc(w_loaded[n], 16)
                if n == 1:
                    sp.dma_start(par[:, C_MLP:C_ALL], small[:, C_MLP:C_ALL]).then_inc(par_loaded, 16)
                if n == 7:
                    load_xt(1, 1)
            for half in range(2):
                sp.dma_start(out_sb[half * ER:(half + 1) * ER, 0, :], bt).then_inc(bt_loaded, 16)
            load_xn(0, 0)
            load_xn(1, 1)

            def step(j, parity, load=True):
                t = 2 * j + parity
                if load:
                    sp.wait_ge(x_lo_ready, t)
                    load_xt(t + 1, 1 - parity)
                sp.wait_ge(evacuated, G * t)
                sp.dma_start(out_t[t - 1], out_sb[:, 1 - parity, :]).then_inc(out_stored[1 - parity], 16)
                if load:
                    load_xn(t + 1, 1 - parity)

            step(0, 1)
            with sp.Fori(1, PAIRS - 1) as j:
                step(j, 0)
                step(j, 1)
            step(PAIRS - 1, 0)
            step(PAIRS - 1, 1, load=False)
            for g in range(G):
                sp.wait_ge(evacuated, G * (TILES - 1) + g + 1)
                cols = slice(OUT0[g], OUT0[g] + OUTN[g])
                sp.dma_start(out_t[TILES - 1][:, cols], out_sb[:, 1, cols]).then_inc(out_stored[1], 16)
            sp.wait_ge(out_stored[0], PAIRS * 16)
            sp.wait_ge(out_stored[1], (PAIRS - 1 + G) * 16)

        @block.gpsimd
        def _(pool):
            nc.gpsimd.memset(ones[:, :], 1.0).then_inc(consts, 1)
            nc.gpsimd.memset(ident32[:, :], 0.0).then_inc(consts, 1)
            nc.gpsimd.memset(group_mask[:, :], 1.0).then_inc(consts, 1)
            nc.gpsimd.memset(ident[:, :], 0.0).then_inc(consts, 1)
            nc.gpsimd.memset(blk_hi[:, :, :].bitcast(U32), 0).then_inc(zeros_ready, 1)
            nc.gpsimd.memset(blk_lo[:, :, :].bitcast(U32), 0).then_inc(zeros_ready, 1)
            pool.wait_ge(consts, 4)
            nc.gpsimd.affine_select(out=ident32[:, :], in_=ident32[:, :], compare_op=ALU.not_equal, fill=1.0,
                                    base=0, pattern=[[-1, BATCH]], channel_multiplier=1).then_inc(consts, 1)
            nc.gpsimd.affine_select(out=group_mask[:, :], in_=group_mask[:, :], compare_op=ALU.is_ge, fill=0.0,
                                    base=0, pattern=[[-K, OG]], channel_multiplier=1).then_inc(consts, 1)
            pool.wait_ge(consts, 6)
            nc.gpsimd.affine_select(out=group_mask[:, :], in_=group_mask[:, :], compare_op=ALU.is_ge, fill=0.0,
                                    base=K - 1, pattern=[[K, OG]], channel_multiplier=-1).then_inc(consts, 1)
            nc.gpsimd.affine_select(out=ident[:, :], in_=ident[:, :], compare_op=ALU.not_equal, fill=1.0,
                                    base=0, pattern=[[-1, P]], channel_multiplier=1).then_inc(consts, 1)
            nc.gpsimd.iota(expert_i[:, :], pattern=[[1, E]], base=0, channel_multiplier=0).then_inc(consts, 1)
            pool.wait_ge(consts, 9)
            nc.gpsimd.tensor_copy(expert_no[:, :], expert_i[:, :]).then_inc(expert_ready, 1)

            def x_low(t, parity):
                pool.wait_ge(x_hi_ready, t + 1)
                nc.gpsimd.tensor_tensor(xt_lo[:, parity, :], xt_raw[:, parity, :],
                                        xt_hi[:, parity, :].bitcast(F32), ALU.subtract).then_inc(x_lo_ready, 1)

            def fold_group(g):
                width = PC * WIDTH[g]
                n0 = PER_G * g
                pool.wait_ge(w_loaded[n0], 16)
                for q in range(1, PER_G):
                    pool.wait_ge(w_loaded[n0 + q], 16)
                    if q > 1:
                        pool.wait_ge(fold_step, n0 + q - 1)
                    nc.gpsimd.tensor_tensor(fold[:, 0:width], piece(w_raw, n0) if q == 1 else fold[:, 0:width],
                                            piece(w_raw, n0 + q), ALU.add).then_inc(fold_step, 1)
                pool.wait_ge(fold_step, n0 + PER_G - 1)
                nc.gpsimd.tensor_tensor(z_cols(w_part, g), fold[:, 0:WIDTH[g]], fold[:, WIDTH[g]:width],
                                        ALU.add).then_inc(fold_step, 1)

            def step(j, parity):
                t = 2 * j + parity
                x_low(t + 1, 1 - parity)

            x_low(0, 0)
            fold_group(0)
            x_low(1, 1)
            fold_group(1)
            step(0, 1)
            with pool.Fori(1, PAIRS - 1) as j:
                step(j, 0)
                step(j, 1)
            step(PAIRS - 1, 0)

        @block.scalar
        def _(act):
            def x_high(j, parity, first=False):
                t = 2 * j + parity
                act.wait_ge(xt_loaded[parity], (j + 1) * 16)
                if not first:
                    act.wait_ge(z_done, G * (t - 1))
                nc.scalar.activation(xt_hi[:, parity, :], xt_raw[:, parity, :], ACT.Copy).then_inc(x_hi_ready, 1)

            def w_high(n):
                act.wait_ge(w_loaded[n], 16)
                nc.scalar.activation(piece(w_hi, n), piece(w_raw, n), ACT.Copy).then_inc(w_hi_ready, 1)

            def z_high(t, g, first=False):
                act.wait_ge(z_done, G * t + g + 1)
                if not first:
                    act.wait_ge(o_done, G * (t - 1) + g + 1)
                nc.scalar.activation(z_cols(z_hi, g), z_ps[g][:, 0:WIDTH[g]], ACT.Copy).then_inc(z_hi_ready, 1)

            def block_high(t, parity, first=False):
                if not first:
                    act.wait_ge(o_done, G * (t - 1))
                for s in range(2):
                    rows = slice(CH * s, CH * (s + 1))
                    nc.scalar.activation(blk_hi[rows, parity, rows],
                                         agg[rows, bass.ds(t, 1), :].rearrange("p t c -> p (t c)"),
                                         ACT.Copy).then_inc(blk_hi_ready, 1)

            def sum_copy(g):
                act.wait_ge(sum_mm, g + 1)
                nc.scalar.activation(z_cols(w_sum, g), s_ps[:, 0:WIDTH[g]], ACT.Copy).then_inc(sum_ready, 1)

            def step(j, parity, last=False):
                t = 2 * j + parity
                z_high(t - 1, 2)
                act.wait_ge(lora_t_mm, t)
                nc.scalar.activation(lora_t[:, :], t_ps[:, 0:P], ACT.Copy).then_inc(lora_t_ready, 1)
                if not last:
                    x_high(j + parity, 1 - parity)
                z_high(t, 0)
                block_high(t, parity)
                z_high(t, 1)
                ratio_exp(t)

            def ratio_exp(t):
                act.wait_ge(gate_step, GATE_STEPS * t + 3)
                nc.scalar.activation(ratio[:, 0:1], top[:, 0:1], ACT.Exp, bias=top[:, 1:2],
                                     scale=-1.0).then_inc(ratio_ready, 1)

            nc.scalar.preload_act_table(ACT.Gelu)
            act.wait_ge(mlp_loaded, 16)
            for layer, at in ((0, C_B0), (1, C_B1)):
                act.wait_ge(mlp_mm, layer + 1)
                nc.scalar.activation(act_g[:, layer, :], s_ps[:, BATCH * layer:BATCH * (layer + 1)], ACT.Gelu,
                                     bias=par[:, at:at + 1]).then_inc(mlp_g, 1)
            nc.scalar.preload_act_table(ACT.Exp)
            act.wait_ge(att_step, 1)
            nc.scalar.activation(att_exp[:, :], s_ps[0:BATCH, 64:64 + K], ACT.Exp, bias=att_max[:, 0:1],
                                 accum_out=att_sum[:, 0:1]).then_inc(att_exped, 1)
            x_high(0, 0, first=True)
            for n in range(PER_G + 1):
                w_high(n)
            for g in range(NG):
                act.wait_ge(agg_mm, g + 1)
                src = (o_ps + [t_ps])[g][0:CH, :].rearrange("p (o t s) -> p t o s", o=OG, s=2)[:, :, :, 0]
                nc.scalar.activation(agg[0:CH, :, OG * g:OG * (g + 1)], src, ACT.Copy).then_inc(agg_ready, 1)
                w_high(PER_G + 1 + g)
            act.wait_ge(zeros_ready, 2)
            act.wait_ge(agg_ready, 2 * NG)
            block_high(0, 0, first=True)
            z_high(0, 0, first=True)
            sum_copy(0)
            x_high(0, 1, first=True)
            for n in range(2 * PER_G + 1, PIECES):
                w_high(n)
            z_high(0, 1, first=True)
            act.wait_ge(consts, 8)
            nc.scalar.activation(ident_r[:, :], ident[:, :], ACT.Copy).then_inc(ident_ready, 1)
            ratio_exp(0)
            act.wait_ge(bt_loaded, 32)
            nc.scalar.activation(b_hi[:, :], out_sb[:, 0, :], ACT.Copy).then_inc(b_hi_ready, 1)
            z_high(0, 2, first=True)
            act.wait_ge(lora_t_mm, 1)
            nc.scalar.activation(lora_t[:, :], t_ps[:, 0:P], ACT.Copy).then_inc(lora_t_ready, 1)
            sum_copy(1)
            sum_copy(2)
            x_high(1, 0)
            z_high(1, 0)
            block_high(1, 1, first=True)
            z_high(1, 1)
            ratio_exp(1)
            with act.Fori(1, PAIRS - 1) as j:
                step(j, 0)
                step(j, 1)
            step(PAIRS - 1, 0)
            step(PAIRS - 1, 1, last=True)
            z_high(TILES - 1, 2)
            act.wait_ge(lora_t_mm, TILES)
            nc.scalar.activation(lora_t[:, :], t_ps[:, 0:P], ACT.Copy).then_inc(lora_t_ready, 1)

        @block.vector
        def _(dve):
            def w_low(n):
                dve.wait_ge(w_hi_ready, n + 1)
                nc.vector.tensor_tensor(piece(w_lo, n), piece(w_raw, n), piece(w_hi, n).bitcast(F32),
                                        ALU.subtract).then_inc(w_lo_ready, 1)

            def z_low(t, g):
                dve.wait_ge(z_hi_ready, G * t + g + 1)
                nc.vector.tensor_tensor(z_cols(z_lo, g), z_ps[g][:, 0:WIDTH[g]], z_cols(z_hi, g).bitcast(F32),
                                        ALU.subtract).then_inc(z_lo_ready, 1)

            def block_low(t, parity):
                dve.wait_ge(blk_hi_ready, 2 * t + 2)
                for s in range(2):
                    rows = slice(CH * s, CH * (s + 1))
                    nc.vector.tensor_tensor(blk_lo[rows, parity, rows],
                                            agg[rows, bass.ds(t, 1), :].rearrange("p t c -> p (t c)"),
                                            blk_hi[rows, parity, rows].bitcast(F32),
                                            ALU.subtract).then_inc(blk_lo_ready, 1)

            def x_bias(j, parity):
                t = 2 * j + parity
                dve.wait_ge(xn_loaded[parity], (j + 1) * 16)
                nc.vector.scalar_tensor_tensor(x_nat[:, parity, :], w_sum[:, GZ:NCOL], bias[:, bass.ds(t, 1)],
                                               x_nat[:, parity, :], ALU.mult, ALU.add).then_inc(x_biased, 1)

            def gating(t, first=False):
                base = GATE_STEPS * t
                dve.wait_ge(o_done, G * t + 1)
                nc.vector.scalar_tensor_tensor(logits[:, :], w_sum[:, 0:E], bias[:, bass.ds(t, 1)],
                                               o_ps[0][:, 0:E], ALU.mult, ALU.add).then_inc(gate_step, 1)
                dve.wait_ge(gate_step, base + 1)
                nc.vector.scalar_tensor_tensor(z_a[:, :], w_sum[:, E:GZ], bias[:, bass.ds(t, 1)],
                                               o_ps[0][:, E:GZ], ALU.mult, ALU.add).then_inc(gate_step, 1)
                nc.vector.max(top[:, :], logits[:, :]).then_inc(gate_step, 1)
                dve.wait_ge(ratio_ready, t + 1)
                nc.vector.tensor_scalar(denom[:, :], ratio[:, :], 1.0, 1.0 / SCALING,
                                        ALU.add, ALU.mult).then_inc(gate_step, 1)
                nc.vector.max_index(top_at[:, :], top[:, :], logits[:, :]).then_inc(gate_step, 1)
                dve.wait_ge(gate_step, base + 4)
                nc.vector.reciprocal(weight[:, 0:1], denom[:, :]).then_inc(gate_step, 1)
                dve.wait_ge(gate_step, base + 5)
                nc.vector.tensor_tensor(onehot[:, :, :], expert_no[:, None, :].to_broadcast([P, 2, E]),
                                        top_at[:, 0:2, None].to_broadcast([P, 2, E]),
                                        ALU.is_equal).then_inc(gate_step, 1)
                dve.wait_ge(gate_step, base + 6)
                nc.vector.tensor_tensor(weight[:, 1:2], weight[:, 0:1], ratio[:, :],
                                        ALU.mult).then_inc(gate_step, 1)
                dve.wait_ge(gate_step, base + 7)
                nc.vector.tensor_scalar(gate_a[:, :], onehot[:, 0, :], weight[:, 0:1], None,
                                        ALU.mult).then_inc(gate_step, 1)
                dve.wait_ge(gate_step, base + 9)
                nc.vector.scalar_tensor_tensor(gate[:, :], onehot[:, 1, :], weight[:, 1:2], gate_a[:, :],
                                               ALU.mult, ALU.add).then_inc(gate_step, 1)
                dve.wait_ge(gate_step, base + 10)
                nc.vector.tensor_tensor(lora[:, :].rearrange("p (e r) -> p e r", r=R),
                                        z_a[:, :].rearrange("p (e r) -> p e r", r=R),
                                        gate[:, :, None].to_broadcast([P, E, R]),
                                        ALU.mult).then_inc(gate_step, 1)
                dve.wait_ge(gate_step, base + 11)
                nc.vector.tensor_copy(lora_split[:, 0, :], lora[:, :]).then_inc(gate_step, 1)
                dve.wait_ge(gate_step, base + 12)
                nc.vector.tensor_tensor(lora_split[:, 1, :], lora[:, :], lora_split[:, 0, :].bitcast(F32),
                                        ALU.subtract).then_inc(gate_step, 1)

            def add_out(j, parity, first=False):
                t = 2 * j + parity
                dve.wait_ge(x_biased, t + 1)
                if not first:
                    dve.wait_ge(out_stored[parity], j * 16)
                for g in range(G):
                    cols = slice(OUT0[g], OUT0[g] + OUTN[g])
                    dve.wait_ge(main_done, G * t + g + 1)
                    nc.vector.tensor_tensor(out_sb[:, parity, cols], o_ps[g][:, SKIP[g]:SKIP[g] + OUTN[g]],
                                            x_nat[:, parity, cols], ALU.add).then_inc(evacuated, 1)

            def step(j, parity, early=False):
                t = 2 * j + parity
                z_low(t - 1, 2)
                x_bias(j, parity)
                z_low(t, 0)
                add_out(j - 1 + parity, 1 - parity, first=early)
                block_low(t, parity)
                z_low(t, 1)
                gating(t)

            dve.wait_ge(mlp_mm, 3)
            nc.vector.tensor_reduce(att_max[:, 0:1], s_ps[0:BATCH, 64:64 + K], AX.X, ALU.max,
                                    negate=True).then_inc(att_step, 1)
            dve.wait_ge(att_exped, 1)
            nc.vector.reciprocal(att_inv[:, :], att_sum[:, :]).then_inc(att_step, 1)
            dve.wait_ge(att_step, 2)
            nc.vector.tensor_scalar(att_rep[:, :, :], att_exp[:, None, :].to_broadcast([BATCH, OG, K]),
                                    att_inv[:, 0:1], None, ALU.mult).then_inc(att_step, 1)
            dve.wait_ge(att_mm, 1)
            nc.vector.tensor_copy(att_t[:, :], s_ps[:, 96:96 + BATCH]).then_inc(att_step, 1)
            dve.wait_ge(att_step, 4)
            dve.wait_ge(consts, 7)
            nc.vector.tensor_tensor(att_diag[:, :, :], group_mask[:, :, None].to_broadcast([P, OG, BATCH]),
                                    att_t[:, None, :].to_broadcast([P, OG, BATCH]),
                                    ALU.mult).then_inc(diag_ready, 1)
            for n in range(PER_G):
                w_low(n)
            dve.wait_ge(bias_mm, 1)
            for s in range(2):
                rows = slice(CH * s, CH * (s + 1))
                src = s_ps[rows, 128:128 + BATCH].rearrange("p (t s) -> p t s", s=2)[:, :, s]
                nc.vector.tensor_copy(bias[rows, :], src).then_inc(bias_ready, 1)
            for g in range(NG):
                dve.wait_ge(agg_mm, g + 1)
                src = (o_ps + [t_ps])[g][CH:P, :].rearrange("p (o t s) -> p t o s", o=OG, s=2)[:, :, :, 1]
                nc.vector.tensor_copy(agg[CH:P, :, OG * g:OG * (g + 1)], src).then_inc(agg_ready, 1)
                w_low(PER_G + g)
            block_low(0, 0)
            z_low(0, 0)
            for n in range(2 * PER_G, PIECES):
                w_low(n)
            z_low(0, 1)
            dve.wait_ge(expert_ready, 1)
            dve.wait_ge(bias_ready, 2)
            dve.wait_ge(sum_ready, 1)
            gating(0)
            g = G - 1
            nc.vector.tensor_reduce(z_cols(w_part, g),
                                    w_raw[:, KC * FIRST[g]:KC * NCOL].rearrange("p (k n) -> p n k", k=KC),
                                    AX.X, ALU.add).then_inc(fold_g2, 1)
            dve.wait_ge(b_hi_ready, 1)
            nc.vector.tensor_tensor(b_lo[:, :], out_sb[:, 0, :], b_hi[:, :].bitcast(F32),
                                    ALU.subtract).then_inc(b_lo_ready, 1)
            z_low(0, 2)
            dve.wait_ge(sum_ready, G)
            x_bias(0, 0)
            z_low(1, 0)
            add_out(0, 0, first=True)
            x_bias(0, 1)
            block_low(1, 1)
            z_low(1, 1)
            gating(1)
            step(1, 0, early=True)
            step(1, 1)
            with dve.Fori(2, PAIRS) as j:
                step(j, 0)
                step(j, 1)
            z_low(TILES - 1, 2)
            add_out(PAIRS - 1, 1)

        @block.tensor
        def _(pe):
            def z_group(t, parity, g, chunks=range(KC), by_piece=False, first=False):
                if not first:
                    pe.wait_ge(z_lo_ready, G * (t - 1) + g + 1)
                for k in chunks:
                    if by_piece and k % PC == 0:
                        pe.wait_ge(w_hi_ready, PER_G * g + k // PC + 1)
                        pe.wait_ge(w_lo_ready, PER_G * g + k // PC + 1)
                    hi = xt_hi[:, parity, k * P:(k + 1) * P]
                    lo = xt_lo[:, parity, k * P:(k + 1) * P]
                    dst = z_ps[g][:, 0:WIDTH[g]]
                    nc.tensor.matmul(dst, hi, w_cols(w_hi, g, k), start=(k == 0), stop=False)
                    nc.tensor.matmul(dst, hi, w_cols(w_lo, g, k), start=False, stop=False)
                    last = nc.tensor.matmul(dst, lo, w_cols(w_hi, g, k), start=False, stop=(k == KC - 1))
                if k == KC - 1:
                    last.then_inc(z_done, 1)

            def o_group(t, parity, g, first=False):
                pe.wait_ge(z_lo_ready, G * t + g + 1)
                if g == 0:
                    pe.wait_ge(blk_lo_ready, 2 * (t + 1))
                if not first:
                    pe.wait_ge(evacuated, G * (t - 1) + g + 1)
                dst = o_ps[g][:, 0:WIDTH[g]]
                nc.tensor.matmul(dst, blk_hi[:, parity, :], z_cols(z_hi, g), start=True, stop=False,
                                 skip_group_check=True)
                nc.tensor.matmul(dst, blk_hi[:, parity, :], z_cols(z_lo, g), start=False, stop=False,
                                 skip_group_check=True)
                nc.tensor.matmul(dst, blk_lo[:, parity, :], z_cols(z_hi, g), start=False, stop=False,
                                 skip_group_check=True).then_inc(o_done, 1)

            def lora_groups(t, groups=range(G)):
                pe.wait_ge(lora_t_ready, t + 1)
                for g in groups:
                    cols = slice(OUT0[g], OUT0[g] + OUTN[g])
                    dst = o_ps[g][:, SKIP[g]:SKIP[g] + OUTN[g]]
                    nc.tensor.matmul(dst, lora_t[:, :], b_hi[:, cols], start=False, stop=False,
                                     skip_group_check=True)
                    nc.tensor.matmul(dst, lora_t[:, :], b_lo[:, cols], start=False, stop=True,
                                     skip_group_check=True).then_inc(main_done, 1)

            def transpose_lora(t):
                pe.wait_ge(gate_step, GATE_STEPS * (t + 1))
                nc.tensor.matmul(t_ps[:, 0:P], lora_split[:, :, :].rearrange("p a c -> p (a c)"), ident_r[:, :],
                                 start=True, stop=True).then_inc(lora_t_mm, 1)

            def step(j, parity):
                t = 2 * j + parity
                pe.wait_ge(x_lo_ready, t + 1)
                z_group(t, parity, 0)
                o_group(t - 1, 1 - parity, 2)
                lora_groups(t - 1)
                z_group(t, parity, 1)
                o_group(t, parity, 0)
                z_group(t, parity, 2)
                o_group(t, parity, 1)
                transpose_lora(t)

            def row_sums(g):
                if g > 0:
                    pe.wait_ge(sum_ready, g)
                nc.tensor.matmul(s_ps[:, 0:WIDTH[g]], ones[:, :], z_cols(w_part, g),
                                 start=True, stop=True).then_inc(sum_mm, 1)

            pe.wait_ge(mlp_loaded, 16)
            nc.tensor.matmul(s_ps[:, 0:BATCH], par[:, C_W0:C_W0 + HID], par[:, C_EMB:C_EMB + BATCH],
                             start=True, stop=True).then_inc(mlp_mm, 1)
            pe.wait_ge(mlp_g, 1)
            nc.tensor.matmul(s_ps[:, BATCH:2 * BATCH], par[:, C_W1:C_W1 + HID], act_g[:, 0, :],
                             start=True, stop=True).then_inc(mlp_mm, 1)
            pe.wait_ge(mlp_g, 2)
            pe.wait_ge(consts, 1)
            nc.tensor.matmul(s_ps[0:BATCH, 64:64 + K], act_g[:, 1, :], par[:, C_W2:C_W2 + K],
                             start=True, stop=False)
            nc.tensor.matmul(s_ps[0:BATCH, 64:64 + K], ones[0:1, 0:BATCH], par[0:1, C_B2:C_B2 + K],
                             start=False, stop=True).then_inc(mlp_mm, 1)
            pe.wait_ge(att_step, 3)
            pe.wait_ge(consts, 5)
            nc.tensor.matmul(s_ps[:, 96:96 + BATCH], att_rep[:, :, :].rearrange("b o k -> b (o k)"),
                             ident32[:, :], start=True, stop=True).then_inc(att_mm, 1)
            pe.wait_ge(x_lo_ready, 1)
            z_group(0, 0, 0, by_piece=True, first=True)
            pe.wait_ge(att_step, 4)
            pe.wait_ge(par_loaded, 16)
            nc.tensor.matmul(s_ps[:, 128:128 + BATCH], par[0:K, C_BK:C_BK + P], att_t[0:K, :],
                             start=True, stop=True).then_inc(bias_mm, 1)
            pe.wait_ge(diag_ready, 1)
            for g in range(NG):
                nc.tensor.matmul((o_ps + [t_ps])[g][:, :], par[:, C_WL + P * g:C_WL + P * (g + 1)],
                                 att_diag[:, :, :].rearrange("p o b -> p (o b)"),
                                 start=True, stop=True).then_inc(agg_mm, 1)
            pe.wait_ge(fold_step, PER_G)
            pe.wait_ge(bias_ready, 2)
            row_sums(0)
            z_group(0, 0, 1, by_piece=True, first=True)
            pe.wait_ge(agg_ready, 2 * NG)
            o_group(0, 0, 0, first=True)
            z_group(0, 0, 2, by_piece=True, first=True)
            o_group(0, 0, 1, first=True)
            pe.wait_ge(ident_ready, 1)
            transpose_lora(0)
            pe.wait_ge(x_lo_ready, 2)
            z_group(1, 1, 0)
            o_group(0, 0, 2, first=True)
            pe.wait_ge(b_lo_ready, 1)
            lora_groups(0)
            pe.wait_ge(fold_step, 2 * PER_G)
            row_sums(1)
            pe.wait_ge(fold_g2, 1)
            row_sums(2)
            z_group(1, 1, 1)
            o_group(1, 1, 0)
            z_group(1, 1, 2)
            o_group(1, 1, 1)
            transpose_lora(1)
            with pe.Fori(1, PAIRS) as j:
                step(j, 0)
                step(j, 1)
            lora_groups(TILES - 1, groups=range(G - 1))
            o_group(TILES - 1, 1, G - 1)
            lora_groups(TILES - 1, groups=range(G - 1, G))


def kernel(**inputs):
    import numpy as np
    import concourse.bacc as bacc
    from concourse import mybir as mb
    from concourse.bass_utils import run_bass_kernel_spmd

    a = {k: np.asarray(v) for k, v in inputs.items()}
    wt = np.concatenate([a["L0_ffn_gate_W"], a["L0_ffn_A"].reshape(ER, D), a["L0_ffn_W_base"]], axis=0).T
    wt = wt.reshape(KC, P, NCOL).transpose(1, 0, 2)
    wext = np.concatenate([wt[:, :, f:f + n].reshape(P, KC * n) for f, n in zip(FIRST, WIDTH)], axis=1)
    bt = a["L0_ffn_B"].transpose(0, 2, 1).reshape(ER, D)
    small = np.zeros((P, C_ALL), np.float32)
    small[:, C_EMB:C_EMB + BATCH] = a["cond_128"].T
    small[:, C_W0:C_W0 + HID] = a["L0_cond_W0"]
    small[:, C_W1:C_W1 + HID] = a["L0_cond_W1"]
    small[:, C_W2:C_W2 + K] = a["L0_cond_W2"]
    small[:, C_B0] = a["L0_cond_b0"]
    small[:, C_B1] = a["L0_cond_b1"]
    small[0, C_B2:C_B2 + K] = a["L0_cond_b2"]
    for s in range(2):
        small[0:K, C_BK + CH * s:C_BK + CH * (s + 1)] = a["L0_cond_bias_k"]
    wl = a["L0_cond_weight"].reshape(K, NG, OG, CH).transpose(2, 0, 1, 3)
    wl = wl.reshape(P, NG, 1, CH)
    small[:, C_WL:C_ALL] = np.concatenate([wl, wl], axis=2).reshape(P, NG * P)

    xt = a["x"].reshape(TILES, P, KC, P).transpose(0, 3, 2, 1).reshape(TILES, P, D)

    nc = bacc.Bacc("TRN2", target_bir_lowering=False, num_devices=1)
    arrays = {"x_in": a["x"], "xt_in": xt, "wext_in": wext, "bt_in": bt, "small_in": small}
    arrays = {k: np.ascontiguousarray(v) for k, v in arrays.items()}
    aps = [nc.dram_tensor(k, v.shape, mb.dt.from_np(v.dtype), kind="ExternalInput").ap() for k, v in arrays.items()]
    out = nc.dram_tensor("out_0", (BATCH, CH, D), mb.dt.float32, kind="ExternalOutput").ap()
    build(nc, *aps, out)
    r = run_bass_kernel_spmd(nc, [arrays], core_ids=[0])
    return r.results[0]["out_0"]
```

```python
import concourse.bass as bass
from concourse import mybir
from contextlib import ExitStack

F32 = mybir.dt.float32
F32R = mybir.dt.float32r
U32 = mybir.dt.uint32
I32 = mybir.dt.int32
ACT = mybir.ActivationFunctionType
ALU = mybir.AluOpType
AX = mybir.AxisListType

P = 128
BATCH, CH, D = 32, 64, 1024
TOK = BATCH * CH
TILES = TOK // P
PAIRS = TILES // 2
KC = D // P
K = 8
E, R = 8, 8
ER = E * R
SCALING = 2.0
HID = 128
GZ = E + ER
OG = P // K // 2
NG = CH // OG
REP = P // K
AGG_BANK = 2

G = 3
WIDTH = [364, 366, 366]
FIRST = [0, 364, 730]
NCOL = GZ + D
assert sum(WIDTH) == NCOL
SKIP = [GZ, 0, 0]
OUT0 = [0, WIDTH[0] - GZ, WIDTH[0] - GZ + WIDTH[1]]
OUTN = [WIDTH[0] - GZ, WIDTH[1], WIDTH[2]]

C_EMB, C_W0, C_W1, C_W2 = 0, 32, 160, 288
C_B0, C_B1, C_B2 = 296, 297, 298
C_MLP = 306
C_BK = 306
C_WL = C_BK + P
C_ALL = C_WL + NG * P

PC = 2
PIECES = G * KC // PC
PER_G = KC // PC


def build(nc, x, xt, wext, bt, small, out):
    x_t = x.rearrange("b c h -> (b c) h").rearrange("(t p) h -> t p h", p=P)
    out_t = out.rearrange("b c h -> (b c) h").rearrange("(t p) h -> t p h", p=P)

    with ExitStack() as ctx:
        def sb(name, shape, dt=F32):
            return ctx.enter_context(nc.sbuf_tensor(name, shape, dt))

        def ps(name):
            return ctx.enter_context(nc.psum_tensor(name, [P, 512], F32))

        def sem(name):
            return ctx.enter_context(nc.semaphore(name))

        w_raw = sb("w_raw", [P, KC * NCOL])
        w_hi = sb("w_hi", [P, KC * NCOL], F32R)
        w_lo = sb("w_lo", [P, KC * NCOL], F32R)
        fold = sb("fold", [P, PC * max(WIDTH)])
        w_part = sb("w_part", [P, NCOL])
        part_hi = sb("part_hi", [P, NCOL], F32R)
        part_lo = sb("part_lo", [P, NCOL], F32R)
        w_sum = sb("w_sum", [P, NCOL])
        b_hi = sb("b_hi", [P, D], F32R)
        b_lo = sb("b_lo", [P, D], F32R)
        xt_raw = sb("xt_raw", [P, 2, D])
        xt_hi = sb("xt_hi", [P, 2, D], F32R)
        xt_lo = sb("xt_lo", [P, 2, D], F32R)
        x_nat = sb("x_nat", [P, 2, D])
        z_hi = sb("z_hi", [P, NCOL], F32R)
        z_lo = sb("z_lo", [P, NCOL], F32R)
        out_sb = sb("out_sb", [P, 2, D])
        agg = sb("agg", [P, TILES, CH])
        blk_hi = sb("blk_hi", [P, 2, P], F32R)
        blk_lo = sb("blk_lo", [P, 2, P], F32R)
        bias = sb("bias", [P, TILES])
        par = sb("par", [P, C_ALL])
        act_g = sb("act_g", [P, 2, BATCH])
        ones = sb("ones", [1, BATCH])
        ones_r = sb("ones_r", [P, P], F32R)
        att_max = sb("att_max", [BATCH, 1])
        att_exp = sb("att_exp", [BATCH, K])
        att_sum = sb("att_sum", [BATCH, 1])
        att_inv = sb("att_inv", [BATCH, 1])
        att_rep = sb("att_rep", [BATCH, REP, K])
        att_t = sb("att_t", [P, BATCH])
        att_diag = sb("att_diag", [P, OG, TILES])
        ident32 = sb("ident32", [BATCH, BATCH])
        group_mask = sb("group_mask", [P, REP])
        ident = sb("ident", [P, P])
        ident_r = sb("ident_r", [P, P], F32R)
        expert_i = sb("expert_i", [P, E], I32)
        expert_no = sb("expert_no", [P, E])
        logits = sb("logits", [P, E])
        z_a = sb("z_a", [P, ER])
        top = sb("top", [P, 8])
        top_at = sb("top_at", [P, 8], U32)
        onehot = sb("onehot", [P, 2, E])
        ratio = sb("ratio", [P, 1])
        denom = sb("denom", [P, 1])
        weight = sb("weight", [P, 2])
        gate_a = sb("gate_a", [P, E])
        gate = sb("gate", [P, E])
        lora = sb("lora", [P, ER])
        lora_split = sb("lora_split", [P, 2, ER], F32R)
        lora_t = sb("lora_t", [P, P], F32R)

        z_ps = [ps(f"z_ps{g}") for g in range(G)]
        o_ps = [ps(f"o_ps{g}") for g in range(G)]
        t_ps = ps("t_ps")
        s_ps = ps("s_ps")

        mlp_loaded = sem("mlp_loaded")
        par_loaded = sem("par_loaded")
        bt_loaded = sem("bt_loaded")
        x0_loaded = [sem("x0_loaded_first"), sem("x0_loaded_second")]
        xt_loaded = [sem("xt_loaded_even"), sem("xt_loaded_odd")]
        xn_loaded = [sem("xn_loaded_even"), sem("xn_loaded_odd")]
        w_loaded = [sem(f"w_loaded{n}") for n in range(PIECES)]
        out_stored = [sem("out_stored_even"), sem("out_stored_odd")]
        consts = sem("consts")
        ones_ready = sem("ones_ready")
        zeros_ready = sem("zeros_ready")
        expert_ready = sem("expert_ready")
        ident_ready = sem("ident_ready")
        mlp_mm = sem("mlp_mm")
        mlp_g = sem("mlp_g")
        att_step = sem("att_step")
        att_exped = sem("att_exped")
        att_mm = sem("att_mm")
        diag_ready = sem("diag_ready")
        bias_mm = sem("bias_mm")
        bias_ready = sem("bias_ready")
        agg_mm = sem("agg_mm")
        agg_ready = sem("agg_ready")
        w0_hi_ready = sem("w0_hi_ready")
        w_hi_ready = sem("w_hi_ready")
        w_lo_ready = sem("w_lo_ready")
        fold_step = sem("fold_step")
        part_hi_ready = sem("part_hi_ready")
        part_lo_ready = sem("part_lo_ready")
        sum_mm = sem("sum_mm")
        sum_ready = sem("sum_ready")
        b_hi_ready = sem("b_hi_ready")
        b_lo_ready = sem("b_lo_ready")
        x_hi_ready = sem("x_hi_ready")
        x_lo_ready = sem("x_lo_ready")
        x0_hi_ready = sem("x0_hi_ready")
        x01_lo_ready = sem("x01_lo_ready")
        x_biased = sem("x_biased")
        z_done = sem("z_done")
        z_hi_ready = sem("z_hi_ready")
        z_lo_ready = sem("z_lo_ready")
        blk_hi_ready = sem("blk_hi_ready")
        blk_lo_ready = sem("blk_lo_ready")
        o_done = sem("o_done")
        gate_step = sem("gate_step")
        ratio_ready = sem("ratio_ready")
        lora_t_mm = sem("lora_t_mm")
        lora_t_ready = sem("lora_t_ready")
        main_done = sem("main_done")
        evacuated = sem("evacuated")

        GATE_STEPS = 13

        def w_cols(w, g, k):
            at = KC * FIRST[g] + k * WIDTH[g]
            return w[:, at:at + WIDTH[g]]

        def piece(w, n):
            g, q = n // PER_G, n % PER_G
            at = KC * FIRST[g] + q * PC * WIDTH[g]
            return w[:, at:at + PC * WIDTH[g]]

        def x_half(half):
            return slice(half * D // 2, (half + 1) * D // 2)

        def z_cols(z, g):
            return z[:, FIRST[g]:FIRST[g] + WIDTH[g]]

        block = ctx.enter_context(nc.Block())

        @block.sync
        def _(sp):
            def load_xt(t, parity):
                sp.dma_start(xt_raw[:, parity, :], xt[t]).then_inc(xt_loaded[parity], 16)

            def load_xn(t, parity):
                sp.dma_start(x_nat[:, parity, :], x_t[t]).then_inc(xn_loaded[parity], 16)

            sp.dma_start(par[:, 0:C_MLP], small[:, 0:C_MLP]).then_inc(mlp_loaded, 16)
            for n in range(PIECES):
                if n < 2:
                    cols = x_half(n)
                    sp.dma_start(xt_raw[:, 0, cols], xt[0][:, cols]).then_inc(x0_loaded[n], 16)
                sp.dma_start(piece(w_raw, n), piece(wext, n)).then_inc(w_loaded[n], 16)
                if n == PER_G - 1:
                    sp.dma_start(par[:, C_MLP:C_ALL], small[:, C_MLP:C_ALL]).then_inc(par_loaded, 16)
            load_xt(1, 1)
            for half in range(2):
                sp.dma_start(out_sb[half * ER:(half + 1) * ER, 0, :], bt).then_inc(bt_loaded, 16)
            load_xn(0, 0)
            load_xn(1, 1)

            for t in range(2):
                sp.wait_ge(x01_lo_ready, 2 * (t + 1))
                load_xt(t + 2, t)

            def step(j, parity, load_t=True, load=True):
                t = 2 * j + parity
                if load_t:
                    sp.wait_ge(x_lo_ready, t - 2)
                    load_xt(t + 1, 1 - parity)
                sp.wait_ge(evacuated, G * t)
                sp.dma_start(out_t[t - 1], out_sb[:, 1 - parity, :]).then_inc(out_stored[1 - parity], 16)
                if load:
                    load_xn(t + 1, 1 - parity)

            step(0, 1, load_t=False)
            step(1, 0, load_t=False)
            step(1, 1)
            with sp.Fori(2, PAIRS - 1) as j:
                step(j, 0)
                step(j, 1)
            step(PAIRS - 1, 0)
            step(PAIRS - 1, 1, load_t=False, load=False)
            for g in range(G):
                sp.wait_ge(evacuated, G * (TILES - 1) + g + 1)
                cols = slice(OUT0[g], OUT0[g] + OUTN[g])
                sp.dma_start(out_t[TILES - 1][:, cols], out_sb[:, 1, cols]).then_inc(out_stored[1], 16)
            sp.wait_ge(out_stored[0], PAIRS * 16)
            sp.wait_ge(out_stored[1], (PAIRS - 1 + G) * 16)

        @block.gpsimd
        def _(pool):
            nc.gpsimd.memset(ones[:, :], 1.0).then_inc(consts, 1)
            nc.gpsimd.memset(ones_r[:, :].bitcast(F32), 1.0).then_inc(ones_ready, 1)
            nc.gpsimd.memset(ident32[:, :], 0.0).then_inc(consts, 1)
            nc.gpsimd.memset(group_mask[:, :], 1.0).then_inc(consts, 1)
            nc.gpsimd.memset(ident[:, :], 0.0).then_inc(consts, 1)
            nc.gpsimd.memset(blk_hi[:, :, :].bitcast(U32), 0).then_inc(zeros_ready, 1)
            nc.gpsimd.memset(blk_lo[:, :, :].bitcast(U32), 0).then_inc(zeros_ready, 1)
            pool.wait_ge(consts, 4)
            nc.gpsimd.affine_select(out=ident32[:, :], in_=ident32[:, :], compare_op=ALU.not_equal, fill=1.0,
                                    base=0, pattern=[[-1, BATCH]], channel_multiplier=1).then_inc(consts, 1)
            nc.gpsimd.affine_select(out=group_mask[:, :], in_=group_mask[:, :], compare_op=ALU.is_ge, fill=0.0,
                                    base=0, pattern=[[-K, REP]], channel_multiplier=1).then_inc(consts, 1)
            pool.wait_ge(consts, 6)
            nc.gpsimd.affine_select(out=group_mask[:, :], in_=group_mask[:, :], compare_op=ALU.is_ge, fill=0.0,
                                    base=K - 1, pattern=[[K, REP]], channel_multiplier=-1).then_inc(consts, 1)
            nc.gpsimd.affine_select(out=ident[:, :], in_=ident[:, :], compare_op=ALU.not_equal, fill=1.0,
                                    base=0, pattern=[[-1, P]], channel_multiplier=1).then_inc(consts, 1)
            nc.gpsimd.iota(expert_i[:, :], pattern=[[1, E]], base=0, channel_multiplier=0).then_inc(consts, 1)
            pool.wait_ge(consts, 9)
            nc.gpsimd.tensor_copy(expert_no[:, :], expert_i[:, :]).then_inc(expert_ready, 1)

            def x_low(t, parity):
                pool.wait_ge(x_hi_ready, t)
                nc.gpsimd.tensor_tensor(xt_lo[:, parity, :], xt_raw[:, parity, :],
                                        xt_hi[:, parity, :].bitcast(F32), ALU.subtract).then_inc(x_lo_ready, 1)

            def fold_group(g):
                width = PC * WIDTH[g]
                n0 = PER_G * g
                pool.wait_ge(w_loaded[n0], 16)
                for q in range(1, PER_G):
                    pool.wait_ge(w_loaded[n0 + q], 16)
                    if q > 1:
                        pool.wait_ge(fold_step, n0 + q - 1)
                    nc.gpsimd.tensor_tensor(fold[:, 0:width], piece(w_raw, n0) if q == 1 else fold[:, 0:width],
                                            piece(w_raw, n0 + q), ALU.add).then_inc(fold_step, 1)
                pool.wait_ge(fold_step, n0 + PER_G - 1)
                nc.gpsimd.tensor_tensor(z_cols(w_part, g), fold[:, 0:WIDTH[g]], fold[:, WIDTH[g]:width],
                                        ALU.add).then_inc(fold_step, 1)
                pool.wait_ge(part_hi_ready, g + 1)
                nc.gpsimd.tensor_tensor(z_cols(part_lo, g), z_cols(w_part, g), z_cols(part_hi, g).bitcast(F32),
                                        ALU.subtract).then_inc(part_lo_ready, 1)

            for g in range(G):
                fold_group(g)
            with pool.Fori(1, PAIRS) as j:
                x_low(2 * j, 0)
                x_low(2 * j + 1, 1)

        @block.scalar
        def _(act):
            def x_high(j, parity, first=False):
                t = 2 * j + parity
                act.wait_ge(xt_loaded[parity], (j + parity) * 16)
                if not first:
                    act.wait_ge(z_done, G * (t - 1))
                nc.scalar.activation(xt_hi[:, parity, :], xt_raw[:, parity, :], ACT.Copy).then_inc(x_hi_ready, 1)

            def w_high(n):
                act.wait_ge(w_loaded[n], 16)
                nc.scalar.activation(piece(w_hi, n), piece(w_raw, n), ACT.Copy).then_inc(w_hi_ready, 1)

            def z_high(t, g, first=False):
                act.wait_ge(z_done, G * t + g + 1)
                if not first:
                    act.wait_ge(o_done, G * (t - 1) + g + 1)
                nc.scalar.activation(z_cols(z_hi, g), z_ps[g][:, 0:WIDTH[g]], ACT.Copy).then_inc(z_hi_ready, 1)

            def block_high(t, parity, first=False):
                if not first:
                    act.wait_ge(o_done, G * (t - 1))
                for s in range(2):
                    rows = slice(CH * s, CH * (s + 1))
                    nc.scalar.activation(blk_hi[rows, parity, rows],
                                         agg[rows, bass.ds(t, 1), :].rearrange("p t c -> p (t c)"),
                                         ACT.Copy).then_inc(blk_hi_ready, 1)

            def part_high(g):
                act.wait_ge(fold_step, PER_G * (g + 1))
                nc.scalar.activation(z_cols(part_hi, g), z_cols(w_part, g), ACT.Copy).then_inc(part_hi_ready, 1)

            def sum_copy(g):
                act.wait_ge(sum_mm, g + 1)
                nc.scalar.activation(z_cols(w_sum, g), s_ps[:, 0:WIDTH[g]], ACT.Copy).then_inc(sum_ready, 1)

            def step(j, parity, last=False):
                t = 2 * j + parity
                z_high(t - 1, 2)
                act.wait_ge(lora_t_mm, t)
                nc.scalar.activation(lora_t[:, :], t_ps[:, 0:P], ACT.Copy).then_inc(lora_t_ready, 1)
                if not last:
                    x_high(j + parity, 1 - parity)
                z_high(t, 0)
                block_high(t, parity)
                if last:
                    ratio_exp(t)
                    z_high(t, 1)
                else:
                    z_high(t, 1)
                    ratio_exp(t)

            def ratio_exp(t):
                act.wait_ge(gate_step, GATE_STEPS * t + 3)
                nc.scalar.activation(ratio[:, 0:1], top[:, 0:1], ACT.Exp, bias=top[:, 1:2],
                                     scale=-1.0).then_inc(ratio_ready, 1)

            nc.scalar.preload_act_table(ACT.Gelu)
            act.wait_ge(mlp_loaded, 16)
            for layer, at in ((0, C_B0), (1, C_B1)):
                act.wait_ge(mlp_mm, layer + 1)
                nc.scalar.activation(act_g[:, layer, :], s_ps[:, BATCH * layer:BATCH * (layer + 1)], ACT.Gelu,
                                     bias=par[:, at:at + 1]).then_inc(mlp_g, 1)
            nc.scalar.preload_act_table(ACT.Exp)
            w_high(1)
            act.wait_ge(att_step, 1)
            nc.scalar.activation(att_exp[:, :], s_ps[0:BATCH, 64:64 + K], ACT.Exp, bias=att_max[:, 0:1],
                                 accum_out=att_sum[:, 0:1]).then_inc(att_exped, 1)
            w_high(2)
            w_high(3)
            w_high(4)
            w_high(5)
            z_high(0, 0, first=True)
            for g in range(NG // AGG_BANK):
                act.wait_ge(agg_mm, g + 1)
                n = AGG_BANK * OG
                src = (o_ps + [t_ps])[g][:, 0:n * TILES].rearrange("p (o t) -> p t o", o=n)
                nc.scalar.activation(agg[:, :, n * g:n * (g + 1)], src, ACT.Copy).then_inc(agg_ready, 1)
                if g < PER_G - 2:
                    w_high(PER_G + g + 2)
                if g == 2:
                    part_high(0)
            act.wait_ge(zeros_ready, 2)
            act.wait_ge(agg_ready, NG // AGG_BANK)
            block_high(0, 0, first=True)
            for n in range(2 * PER_G, PIECES):
                w_high(n)
                if n == 2 * PER_G + 2:
                    z_high(0, 1, first=True)
            sum_copy(0)
            x_high(0, 1, first=True)
            act.wait_ge(consts, 8)
            nc.scalar.activation(ident_r[:, :], ident[:, :], ACT.Copy).then_inc(ident_ready, 1)
            ratio_exp(0)
            part_high(1)
            act.wait_ge(bt_loaded, 32)
            nc.scalar.activation(b_hi[:, :], out_sb[:, 0, :], ACT.Copy).then_inc(b_hi_ready, 1)
            z_high(0, 2, first=True)
            act.wait_ge(lora_t_mm, 1)
            nc.scalar.activation(lora_t[:, :], t_ps[:, 0:P], ACT.Copy).then_inc(lora_t_ready, 1)
            sum_copy(1)
            x_high(1, 0)
            block_high(1, 1, first=True)
            z_high(1, 0)
            part_high(2)
            z_high(1, 1)
            ratio_exp(1)
            sum_copy(2)
            with act.Fori(1, PAIRS - 1) as j:
                step(j, 0)
                step(j, 1)
            step(PAIRS - 1, 0)
            step(PAIRS - 1, 1, last=True)
            act.wait_ge(lora_t_mm, TILES)
            nc.scalar.activation(lora_t[:, :], t_ps[:, 0:P], ACT.Copy).then_inc(lora_t_ready, 1)
            z_high(TILES - 1, 2)

        @block.vector
        def _(dve):
            def x_low(t, half):
                cols = x_half(half)
                nc.vector.tensor_tensor(xt_lo[:, t, cols], xt_raw[:, t, cols],
                                        xt_hi[:, t, cols].bitcast(F32), ALU.subtract).then_inc(x01_lo_ready, 1)

            def w_low(n):
                dve.wait_ge(w0_hi_ready if n == 0 else w_hi_ready, max(n, 1))
                nc.vector.tensor_tensor(piece(w_lo, n), piece(w_raw, n), piece(w_hi, n).bitcast(F32),
                                        ALU.subtract).then_inc(w_lo_ready, 1)

            def z_low(t, g):
                dve.wait_ge(z_hi_ready, G * t + g + 1)
                nc.vector.tensor_tensor(z_cols(z_lo, g), z_ps[g][:, 0:WIDTH[g]], z_cols(z_hi, g).bitcast(F32),
                                        ALU.subtract).then_inc(z_lo_ready, 1)

            def block_low(t, parity):
                dve.wait_ge(blk_hi_ready, 2 * t + 2)
                for s in range(2):
                    rows = slice(CH * s, CH * (s + 1))
                    nc.vector.tensor_tensor(blk_lo[rows, parity, rows],
                                            agg[rows, bass.ds(t, 1), :].rearrange("p t c -> p (t c)"),
                                            blk_hi[rows, parity, rows].bitcast(F32),
                                            ALU.subtract).then_inc(blk_lo_ready, 1)

            def x_bias(j, parity, cols=slice(0, D)):
                t = 2 * j + parity
                dve.wait_ge(xn_loaded[parity], (j + 1) * 16)
                nc.vector.scalar_tensor_tensor(x_nat[:, parity, cols], w_sum[:, GZ + cols.start:GZ + cols.stop],
                                               bias[:, bass.ds(t, 1)], x_nat[:, parity, cols],
                                               ALU.mult, ALU.add).then_inc(x_biased, 1)

            def gating(t):
                base = GATE_STEPS * t
                dve.wait_ge(o_done, G * t + 1)
                nc.vector.scalar_tensor_tensor(logits[:, :], w_sum[:, 0:E], bias[:, bass.ds(t, 1)],
                                               o_ps[0][:, 0:E], ALU.mult, ALU.add).then_inc(gate_step, 1)
                dve.wait_ge(gate_step, base + 1)
                nc.vector.scalar_tensor_tensor(z_a[:, :], w_sum[:, E:GZ], bias[:, bass.ds(t, 1)],
                                               o_ps[0][:, E:GZ], ALU.mult, ALU.add).then_inc(gate_step, 1)
                nc.vector.max(top[:, :], logits[:, :]).then_inc(gate_step, 1)
                dve.wait_ge(ratio_ready, t + 1)
                nc.vector.tensor_scalar(denom[:, :], ratio[:, :], 1.0, 1.0 / SCALING,
                                        ALU.add, ALU.mult).then_inc(gate_step, 1)
                nc.vector.max_index(top_at[:, :], top[:, :], logits[:, :]).then_inc(gate_step, 1)
                dve.wait_ge(gate_step, base + 4)
                nc.vector.reciprocal(weight[:, 0:1], denom[:, :]).then_inc(gate_step, 1)
                dve.wait_ge(gate_step, base + 5)
                nc.vector.tensor_tensor(onehot[:, :, :], expert_no[:, None, :].to_broadcast([P, 2, E]),
                                        top_at[:, 0:2, None].to_broadcast([P, 2, E]),
                                        ALU.is_equal).then_inc(gate_step, 1)
                dve.wait_ge(gate_step, base + 6)
                nc.vector.tensor_tensor(weight[:, 1:2], weight[:, 0:1], ratio[:, :],
                                        ALU.mult).then_inc(gate_step, 1)
                dve.wait_ge(gate_step, base + 7)
                nc.vector.tensor_scalar(gate_a[:, :], onehot[:, 0, :], weight[:, 0:1], None,
                                        ALU.mult).then_inc(gate_step, 1)
                dve.wait_ge(gate_step, base + 9)
                nc.vector.scalar_tensor_tensor(gate[:, :], onehot[:, 1, :], weight[:, 1:2], gate_a[:, :],
                                               ALU.mult, ALU.add).then_inc(gate_step, 1)
                dve.wait_ge(gate_step, base + 10)
                nc.vector.tensor_tensor(lora[:, :].rearrange("p (e r) -> p e r", r=R),
                                        z_a[:, :].rearrange("p (e r) -> p e r", r=R),
                                        gate[:, :, None].to_broadcast([P, E, R]),
                                        ALU.mult).then_inc(gate_step, 1)
                dve.wait_ge(gate_step, base + 11)
                nc.vector.tensor_copy(lora_split[:, 0, :], lora[:, :]).then_inc(gate_step, 1)
                dve.wait_ge(gate_step, base + 12)
                nc.vector.tensor_tensor(lora_split[:, 1, :], lora[:, :], lora_split[:, 0, :].bitcast(F32),
                                        ALU.subtract).then_inc(gate_step, 1)

            def add_out(j, parity, first=False, groups=range(G)):
                t = 2 * j + parity
                dve.wait_ge(x_biased, t + G)
                if not first:
                    dve.wait_ge(out_stored[parity], j * 16)
                for g in groups:
                    cols = slice(OUT0[g], OUT0[g] + OUTN[g])
                    dve.wait_ge(main_done, G * t + g + 1)
                    nc.vector.tensor_tensor(out_sb[:, parity, cols], o_ps[g][:, SKIP[g]:SKIP[g] + OUTN[g]],
                                            x_nat[:, parity, cols], ALU.add).then_inc(evacuated, 1)

            def step(j, parity, early=False, last=False):
                t = 2 * j + parity
                z_low(t - 1, 2)
                x_bias(j, parity)
                z_low(t, 0)
                block_low(t, parity)
                add_out(j - 1 + parity, 1 - parity, first=early)
                if last:
                    gating(t)
                    z_low(t, 1)
                else:
                    z_low(t, 1)
                    gating(t)

            def x0_high(half):
                cols = x_half(half)
                dve.wait_ge(x0_loaded[half], 16)
                nc.vector.tensor_copy(xt_hi[:, 0, cols], xt_raw[:, 0, cols]).then_inc(x0_hi_ready, 1)
                dve.wait_ge(x0_hi_ready, half + 1)

            x0_high(0)
            x_low(0, 0)
            dve.wait_ge(w_loaded[0], 16)
            nc.vector.tensor_copy(piece(w_hi, 0), piece(w_raw, 0)).then_inc(w0_hi_ready, 1)
            w_low(0)
            dve.wait_ge(mlp_mm, 3)
            nc.vector.tensor_reduce(att_max[:, 0:1], s_ps[0:BATCH, 64:64 + K], AX.X, ALU.max,
                                    negate=True).then_inc(att_step, 1)
            x0_high(1)
            x_low(0, 1)
            w_low(1)
            dve.wait_ge(att_exped, 1)
            nc.vector.reciprocal(att_inv[:, :], att_sum[:, :]).then_inc(att_step, 1)
            dve.wait_ge(att_step, 2)
            nc.vector.tensor_scalar(att_rep[:, :, :], att_exp[:, None, :].to_broadcast([BATCH, REP, K]),
                                    att_inv[:, 0:1], None, ALU.mult).then_inc(att_step, 1)
            w_low(2)
            w_low(3)
            dve.wait_ge(att_mm, 1)
            nc.vector.tensor_copy(att_t[:, :], s_ps[:, 96:96 + BATCH]).then_inc(att_step, 1)
            dve.wait_ge(att_step, 4)
            dve.wait_ge(consts, 7)
            for s in range(2):
                rows = slice(CH * s, CH * (s + 1))
                att_s = att_t[rows, :].rearrange("p (t s) -> p t s", s=2)[:, :, s]
                nc.vector.tensor_tensor(att_diag[rows, :, :],
                                        group_mask[rows, OG * s:OG * (s + 1), None].to_broadcast([CH, OG, TILES]),
                                        att_s[:, None, :].to_broadcast([CH, OG, TILES]),
                                        ALU.mult).then_inc(diag_ready, 1)
            w_low(PER_G)
            dve.wait_ge(bias_mm, 1)
            for s in range(2):
                rows = slice(CH * s, CH * (s + 1))
                src = s_ps[rows, 128:128 + BATCH].rearrange("p (t s) -> p t s", s=2)[:, :, s]
                nc.vector.tensor_copy(bias[rows, :], src).then_inc(bias_ready, 1)
            z_low(0, 0)
            for n in range(PER_G + 1, 2 * PER_G):
                w_low(n)
            block_low(0, 0)
            for n in range(2 * PER_G, PIECES):
                w_low(n)
                if n == 2 * PER_G + 2:
                    z_low(0, 1)
            dve.wait_ge(x_hi_ready, 1)
            x_low(1, 0)
            x_low(1, 1)
            dve.wait_ge(expert_ready, 1)
            dve.wait_ge(bias_ready, 2)
            dve.wait_ge(sum_ready, 1)
            gating(0)
            dve.wait_ge(b_hi_ready, 1)
            nc.vector.tensor_tensor(b_lo[:, :], out_sb[:, 0, :], b_hi[:, :].bitcast(F32),
                                    ALU.subtract).then_inc(b_lo_ready, 1)

            def first_tile_out(g):
                cols = slice(OUT0[g], OUT0[g] + OUTN[g])
                dve.wait_ge(sum_ready, g + 1)
                x_bias(0, 0, cols)
                dve.wait_ge(x_biased, g + 1)
                dve.wait_ge(main_done, g + 1)
                nc.vector.tensor_tensor(out_sb[:, 0, cols], o_ps[g][:, SKIP[g]:SKIP[g] + OUTN[g]],
                                        x_nat[:, 0, cols], ALU.add).then_inc(evacuated, 1)

            z_low(0, 2)
            block_low(1, 1)
            z_low(1, 0)
            first_tile_out(0)
            first_tile_out(1)
            z_low(1, 1)
            gating(1)
            first_tile_out(2)
            x_bias(0, 1)
            step(1, 0, early=True)
            step(1, 1)
            with dve.Fori(2, PAIRS - 1) as j:
                step(j, 0)
                step(j, 1)
            step(PAIRS - 1, 0)
            step(PAIRS - 1, 1, last=True)
            add_out(PAIRS - 1, 1, groups=range(1))
            z_low(TILES - 1, G - 1)
            add_out(PAIRS - 1, 1, groups=range(1, G - 1))
            cols = slice(OUT0[G - 1], D)
            dve.wait_ge(o_done, G * TILES)
            nc.vector.tensor_tensor(out_sb[:, 1, cols], o_ps[G - 1][:, 0:WIDTH[G - 1]], x_nat[:, 1, cols],
                                    ALU.add).then_inc(evacuated, 1)

        @block.tensor
        def _(pe):
            def z_group(t, parity, g, chunks=range(KC), by_piece=False, bank_free=False):
                if not bank_free:
                    pe.wait_ge(z_lo_ready, G * (t - 1) + g + 1)
                for k in chunks:
                    if by_piece and k % PC == 0:
                        pe.wait_ge(w_lo_ready, PER_G * g + k // PC + 1)
                    hi = xt_hi[:, parity, k * P:(k + 1) * P]
                    lo = xt_lo[:, parity, k * P:(k + 1) * P]
                    dst = z_ps[g][:, 0:WIDTH[g]]
                    nc.tensor.matmul(dst, hi, w_cols(w_hi, g, k), start=(k == 0), stop=False)
                    nc.tensor.matmul(dst, hi, w_cols(w_lo, g, k), start=False, stop=False)
                    last = nc.tensor.matmul(dst, lo, w_cols(w_hi, g, k), start=False, stop=(k == KC - 1))
                if k == KC - 1:
                    last.then_inc(z_done, 1)

            def o_group(t, parity, g, bank_free=False, start=True):
                pe.wait_ge(z_hi_ready, G * t + g + 1)
                if g == 0:
                    pe.wait_ge(blk_lo_ready, 2 * (t + 1))
                if not bank_free:
                    pe.wait_ge(evacuated, G * (t - 1) + g + 1)
                dst = o_ps[g][:, 0:WIDTH[g]]
                nc.tensor.matmul(dst, blk_hi[:, parity, :], z_cols(z_hi, g), start=start, stop=False,
                                 skip_group_check=True)
                nc.tensor.matmul(dst, blk_lo[:, parity, :], z_cols(z_hi, g), start=False, stop=False,
                                 skip_group_check=True)
                pe.wait_ge(z_lo_ready, G * t + g + 1)
                nc.tensor.matmul(dst, blk_hi[:, parity, :], z_cols(z_lo, g), start=False, stop=not start,
                                 skip_group_check=True).then_inc(o_done, 1)

            def lora_groups(t, groups=range(G)):
                pe.wait_ge(lora_t_ready, t + 1)
                for g in groups:
                    cols = slice(OUT0[g], OUT0[g] + OUTN[g])
                    dst = o_ps[g][:, SKIP[g]:SKIP[g] + OUTN[g]]
                    nc.tensor.matmul(dst, lora_t[:, :], b_hi[:, cols], start=False, stop=False,
                                     skip_group_check=True)
                    nc.tensor.matmul(dst, lora_t[:, :], b_lo[:, cols], start=False, stop=True,
                                     skip_group_check=True).then_inc(main_done, 1)

            def transpose_lora(t):
                pe.wait_ge(gate_step, GATE_STEPS * (t + 1))
                nc.tensor.matmul(t_ps[:, 0:P], lora_split[:, :, :].rearrange("p a c -> p (a c)"), ident_r[:, :],
                                 start=True, stop=True).then_inc(lora_t_mm, 1)

            def step(j, parity):
                t = 2 * j + parity
                pe.wait_ge(x_lo_ready, t - 1)
                z_group(t, parity, 0)
                o_group(t - 1, 1 - parity, 2)
                lora_groups(t - 1)
                z_group(t, parity, 1)
                o_group(t, parity, 0)
                z_group(t, parity, 2)
                o_group(t, parity, 1)
                transpose_lora(t)

            def row_sums(g):
                if g > 0:
                    pe.wait_ge(sum_ready, g)
                pe.wait_ge(part_lo_ready, g + 1)
                nc.tensor.matmul(s_ps[:, 0:WIDTH[g]], ones_r[:, :], z_cols(part_hi, g), start=True, stop=False)
                nc.tensor.matmul(s_ps[:, 0:WIDTH[g]], ones_r[:, :], z_cols(part_lo, g),
                                 start=False, stop=True).then_inc(sum_mm, 1)

            def warm(n):
                for _ in range(n):
                    nc.tensor.matmul(t_ps[:, :], ones_r[:, :], ones_r[:, None, :].to_broadcast([P, 4, P]),
                                     start=True, stop=True)

            pe.wait_ge(ones_ready, 1)
            warm(5)
            pe.wait_ge(mlp_loaded, 16)
            nc.tensor.matmul(s_ps[:, 0:BATCH], par[:, C_W0:C_W0 + HID], par[:, C_EMB:C_EMB + BATCH],
                             start=True, stop=True).then_inc(mlp_mm, 1)
            warm(1)
            pe.wait_ge(mlp_g, 1)
            nc.tensor.matmul(s_ps[:, BATCH:2 * BATCH], par[:, C_W1:C_W1 + HID], act_g[:, 0, :],
                             start=True, stop=True).then_inc(mlp_mm, 1)
            warm(2)
            pe.wait_ge(mlp_g, 2)
            pe.wait_ge(consts, 1)
            nc.tensor.matmul(s_ps[0:BATCH, 64:64 + K], act_g[:, 1, :], par[:, C_W2:C_W2 + K],
                             start=True, stop=False)
            nc.tensor.matmul(s_ps[0:BATCH, 64:64 + K], ones[:, :], par[0:1, C_B2:C_B2 + K],
                             start=False, stop=True).then_inc(mlp_mm, 1)
            warm(1)
            pe.wait_ge(x01_lo_ready, 1)
            z_group(0, 0, 0, chunks=range(PC + 1), by_piece=True, bank_free=True)
            pe.wait_ge(att_step, 3)
            pe.wait_ge(consts, 5)
            nc.tensor.matmul(s_ps[:, 96:96 + BATCH], att_rep[:, :, :].rearrange("b o k -> b (o k)"),
                             ident32[:, :], start=True, stop=True).then_inc(att_mm, 1)
            z_group(0, 0, 0, chunks=range(PC + 1, KC // 2), by_piece=True, bank_free=True)
            pe.wait_ge(x01_lo_ready, 2)
            z_group(0, 0, 0, chunks=range(KC // 2, KC), by_piece=True, bank_free=True)
            pe.wait_ge(att_step, 4)
            pe.wait_ge(par_loaded, 16)
            nc.tensor.matmul(s_ps[:, 128:128 + BATCH], par[0:K, C_BK:C_BK + P], att_t[0:K, :],
                             start=True, stop=True).then_inc(bias_mm, 1)
            pe.wait_ge(diag_ready, 2)
            for g in range(NG):
                bank = (o_ps + [t_ps])[g // AGG_BANK]
                at = g % AGG_BANK * OG * TILES
                mm = nc.tensor.matmul(bank[:, at:at + OG * TILES], par[:, C_WL + P * g:C_WL + P * (g + 1)],
                                      att_diag[:, :, :].rearrange("p o t -> p (o t)"), start=True, stop=True)
                if g % AGG_BANK == AGG_BANK - 1:
                    mm.then_inc(agg_mm, 1)
            z_group(0, 0, 1, by_piece=True, bank_free=True)
            pe.wait_ge(bias_ready, 2)
            row_sums(0)
            pe.wait_ge(agg_ready, NG // AGG_BANK)
            o_group(0, 0, 0, bank_free=True)
            z_group(0, 0, 2, by_piece=True, bank_free=True)
            o_group(0, 0, 1, bank_free=True)
            pe.wait_ge(x01_lo_ready, 4)
            z_group(1, 1, 0, chunks=range(KC - 2))
            pe.wait_ge(ident_ready, 1)
            transpose_lora(0)
            row_sums(1)
            z_group(1, 1, 0, chunks=range(KC - 2, KC), bank_free=True)
            o_group(0, 0, 2, bank_free=True)
            pe.wait_ge(b_lo_ready, 1)
            lora_groups(0)
            z_group(1, 1, 1)
            o_group(1, 1, 0)
            z_group(1, 1, 2, chunks=range(KC // 2))
            row_sums(2)
            z_group(1, 1, 2, chunks=range(KC // 2, KC), bank_free=True)
            o_group(1, 1, 1)
            transpose_lora(1)
            with pe.Fori(1, PAIRS - 1) as j:
                step(j, 0)
                step(j, 1)
            step(PAIRS - 1, 0)
            t = TILES - 1
            pe.wait_ge(x_lo_ready, t - 1)
            z_group(t, 1, 0)
            o_group(t - 1, 0, 2)
            lora_groups(t - 1)
            z_group(t, 1, 1, chunks=range(KC // 2))
            o_group(t, 1, 0)
            z_group(t, 1, 1, chunks=range(KC // 2, KC), bank_free=True)
            z_group(t, 1, 2, chunks=range(KC // 2))
            o_group(t, 1, 1)
            transpose_lora(t)
            z_group(t, 1, 2, chunks=range(KC // 2, KC), bank_free=True)
            lora_groups(t, groups=range(G - 1))
            pe.wait_ge(evacuated, G * t)
            dst = o_ps[G - 1][:, 0:WIDTH[G - 1]]
            nc.tensor.matmul(dst, lora_t[:, :], b_hi[:, OUT0[G - 1]:D], start=True, stop=False,
                             skip_group_check=True)
            nc.tensor.matmul(dst, lora_t[:, :], b_lo[:, OUT0[G - 1]:D], start=False, stop=False,
                             skip_group_check=True)
            o_group(t, 1, G - 1, start=False)


def kernel(**inputs):
    import numpy as np
    import concourse.bacc as bacc
    from concourse import mybir as mb
    from concourse.bass_utils import run_bass_kernel_spmd

    a = {k: np.asarray(v) for k, v in inputs.items()}
    wt = np.concatenate([a["L0_ffn_gate_W"], a["L0_ffn_A"].reshape(ER, D), a["L0_ffn_W_base"]], axis=0).T
    wt = wt.reshape(KC, P, NCOL).transpose(1, 0, 2)
    wext = np.concatenate([wt[:, :, f:f + n].reshape(P, KC * n) for f, n in zip(FIRST, WIDTH)], axis=1)
    bt = a["L0_ffn_B"].transpose(0, 2, 1).reshape(ER, D)
    small = np.zeros((P, C_ALL), np.float32)
    small[:, C_EMB:C_EMB + BATCH] = a["cond_128"].T
    small[:, C_W0:C_W0 + HID] = a["L0_cond_W0"]
    small[:, C_W1:C_W1 + HID] = a["L0_cond_W1"]
    small[:, C_W2:C_W2 + K] = a["L0_cond_W2"]
    small[:, C_B0] = a["L0_cond_b0"]
    small[:, C_B1] = a["L0_cond_b1"]
    small[0, C_B2:C_B2 + K] = a["L0_cond_b2"]
    for s in range(2):
        small[0:K, C_BK + CH * s:C_BK + CH * (s + 1)] = a["L0_cond_bias_k"]
    wl = a["L0_cond_weight"].reshape(K, NG, OG, CH).transpose(2, 0, 1, 3).reshape(CH, NG, CH)
    for s in range(2):
        view = small[CH * s:CH * (s + 1), C_WL:C_ALL]
        for g in range(NG):
            view[:, P * g + CH * s:P * g + CH * (s + 1)] = wl[:, g]

    xt = a["x"].reshape(TILES, P, KC, P).transpose(0, 3, 2, 1).reshape(TILES, P, D)

    nc = bacc.Bacc("TRN2", target_bir_lowering=False, num_devices=1)
    arrays = {"x_in": a["x"], "xt_in": xt, "wext_in": wext, "bt_in": bt, "small_in": small}
    arrays = {k: np.ascontiguousarray(v) for k, v in arrays.items()}
    aps = [nc.dram_tensor(k, v.shape, mb.dt.from_np(v.dtype), kind="ExternalInput").ap() for k, v in arrays.items()]
    out = nc.dram_tensor("out_0", (BATCH, CH, D), mb.dt.float32, kind="ExternalOutput").ap()
    build(nc, *aps, out)
    r = run_bass_kernel_spmd(nc, [arrays], core_ids=[0])
    return r.results[0]["out_0"]
```
